# Optimizing a Trainium2 kernel written in Bass

```python
import numpy as np
import jax
import jax.numpy as jnp

def _softmax(x, axis=-1):
    return jax.nn.softmax(x, axis=axis)

def _gelu(x):
    return jax.nn.gelu(x, approximate=True)

def _silu(x):
    return jax.nn.silu(x)

def _sigmoid(x):
    return jax.nn.sigmoid(x)

def _layernorm(x, axis=-1, eps=1e-05):
    m = jnp.mean(x, axis=axis, keepdims=True)
    v = jnp.var(x, axis=axis, keepdims=True)
    return (x - m) / jnp.sqrt(v + eps)

def _scatter_add(tgt, idx, src, axis=0):
    return tgt.at[idx].add(src)

def _segment_sum(src, seg, n):
    return jax.ops.segment_sum(src, seg, n)
kernel_name = 'mk_xattn_ffn_d1_seqx_r4_661899'

def setup_inputs(seed: int=0):
    np.random.seed(seed)
    _w = jnp.asarray

    def _rec_inputs():
        import jax
        import jax.numpy as jnp
        _rk = jax.random.key(seed)
        x = -0.000125 + 0.9999 * jax.random.normal(jax.random.fold_in(_rk, 1), (4, 512, 512), jnp.float32)
        _lenS = 512 - jax.random.randint(jax.random.fold_in(_rk, 7), (4,), 0, max(1, 512 // 4) + 1, jnp.int32)
        _lenS2 = 512 - jax.random.randint(jax.random.fold_in(_rk, 8), (4,), 0, max(1, 512 // 4) + 1, jnp.int32)
        itok_BxS_13_99985 = jax.random.randint(jax.random.fold_in(_rk, 11), (4, 512), 13, 99986, jnp.int32)
        _ctx_2048P = jax.random.normal(jax.random.fold_in(_rk, 12), (4, 16, 512), jnp.float32)
        _ctx_2048c = jax.random.dirichlet(jax.random.fold_in(_rk, 512), 0.3 * jnp.ones((16,), jnp.float32), (4, 512))
        _ctx_2048t = jnp.einsum('bsk,bkd->bsd', _ctx_2048c, _ctx_2048P)
        _ctx_2048t = _ctx_2048t * jax.lax.rsqrt(jnp.mean(jnp.square(_ctx_2048t)) + 1e-12) * 0.953939
        ctx_2048 = 6.82029e-06 + 0.0200006 * (_ctx_2048t + 0.3 * jax.random.normal(jax.random.fold_in(_rk, 612), (4, 512, 512), jnp.float32))
        return (x, itok_BxS_13_99985, ctx_2048)
    x, itok_BxS_13_99985, ctx_2048 = _rec_inputs()

    def _L0_xattn_setup():
        import jax, jax.numpy as jnp
        import numpy as np
        B, S, D = (4, 1024, 512)
        E = 4
        F = 2048 // E
        VOCAB = 25000
        key = jax.random.key(seed)
        k1, k2, k3, k4, k5 = jax.random.split(key, 5)
        hidden_states = jax.random.normal(k1, (B, S, D), dtype=jnp.float32)
        token_ids = jax.random.randint(k2, (B, S), 0, VOCAB, dtype=jnp.int64)
        Wg = jax.random.normal(k3, (E, F, D), dtype=jnp.float32) * 0.02
        Wu = jax.random.normal(k4, (E, F, D), dtype=jnp.float32) * 0.02
        Wd = jax.random.normal(k5, (E, D, F), dtype=jnp.float32) * 0.02
        return {'hidden_states': hidden_states, 'token_ids': token_ids, 'Wg': Wg, 'Wu': Wu, 'Wd': Wd}
    _L0_xattn_all = _L0_xattn_setup()
    _L0_xattn_in = {k: v for k, v in _L0_xattn_all.items() if k in ()}
    del _L0_xattn_all

    def _L0_ffn_setup():
        import jax, jax.numpy as jnp
        import numpy as np
        B, S, H = (2, 512, 512)
        E, K = (16, 4)
        I_MOE, I_SH = (352, 1408)
        key = jax.random.key(seed)
        ks = jax.random.split(key, 9)

        def w(k, shape, fan_in):
            return jax.random.normal(k, shape, jnp.float32) * fan_in ** (-0.5)
        return {'hidden_states': jax.random.normal(ks[0], (B, S, H), jnp.float32), 'router_w': w(ks[1], (E, H), H), 'w_gate': w(ks[2], (E, H, I_MOE), H), 'w_up': w(ks[3], (E, H, I_MOE), H), 'w_down': w(ks[4], (E, I_MOE, H), I_MOE), 'sh_gate': w(ks[5], (H, I_SH), H), 'sh_up': w(ks[6], (H, I_SH), H), 'sh_down': w(ks[7], (I_SH, H), I_SH), 'sh_gate_w': w(ks[8], (H, 1), H)}
    _L0_ffn_all = _L0_ffn_setup()
    _L0_ffn_in = {k: v for k, v in _L0_ffn_all.items() if k in ('router_w', 'w_gate', 'w_up', 'w_down', 'sh_gate', 'sh_up', 'sh_down', 'sh_gate_w')}
    del _L0_ffn_all
    return {'x': x, 'itok_BxS_13_99985': itok_BxS_13_99985, 'ctx_2048': ctx_2048, 'L0_ffn_router_w': _L0_ffn_in['router_w'], 'L0_ffn_w_gate': _L0_ffn_in['w_gate'], 'L0_ffn_w_up': _L0_ffn_in['w_up'], 'L0_ffn_w_down': _L0_ffn_in['w_down'], 'L0_ffn_sh_gate': _L0_ffn_in['sh_gate'], 'L0_ffn_sh_up': _L0_ffn_in['sh_up'], 'L0_ffn_sh_down': _L0_ffn_in['sh_down'], 'L0_ffn_sh_gate_w': _L0_ffn_in['sh_gate_w']}

def reference(x, itok_BxS_13_99985, ctx_2048, L0_ffn_router_w, L0_ffn_w_gate, L0_ffn_w_up, L0_ffn_w_down, L0_ffn_sh_gate, L0_ffn_sh_up, L0_ffn_sh_down, L0_ffn_sh_gate_w):
    import jax
    import jax.numpy as jnp

    def _L0_xattn_ref(hidden_states, token_ids, Wg, Wu, Wd):
        import jax, jax.numpy as jnp
        import numpy as np
        B, S, D = (4, 1024, 512)
        E = 4
        F = 2048 // E
        VOCAB = 25000
        tokens_per_expert = VOCAB // E
        tid = jnp.clip(token_ids, 0, VOCAB - 1)
        expert_ids = jnp.minimum(tid // tokens_per_expert, E - 1)
        out = jnp.zeros_like(hidden_states)
        for e in range(E):
            g = jax.nn.silu(jnp.einsum('bsd,fd->bsf', hidden_states, Wg[e]))
            u = jnp.einsum('bsd,fd->bsf', hidden_states, Wu[e])
            y = jnp.einsum('bsf,df->bsd', g * u, Wd[e])
            out = jnp.where((expert_ids == e)[..., None], y, out)
        return out

    def _L0_ffn_ref(hidden_states, router_w, w_gate, w_up, w_down, sh_gate, sh_up, sh_down, sh_gate_w):
        import jax, jax.numpy as jnp
        import numpy as np
        B, S, H = (2, 512, 512)
        E, K = (16, 4)
        I_MOE, I_SH = (352, 1408)
        orig = hidden_states.shape
        h = hidden_states.reshape(-1, orig[-1])
        N = h.shape[0]
        logits = h @ router_w.T
        probs = jax.nn.softmax(logits.astype(jnp.float32), axis=-1)
        top_vals, top_idx = jax.lax.top_k(probs, K)
        top_vals = top_vals / jnp.maximum(top_vals.sum(-1, keepdims=True), 1e-09)
        top_vals = top_vals.astype(h.dtype)
        comb = jnp.zeros((N, E), h.dtype).at[jnp.arange(N)[:, None], top_idx].add(top_vals)
        g = jnp.einsum('nh,ehi->eni', h, w_gate)
        u = jnp.einsum('nh,ehi->eni', h, w_up)
        y = jnp.einsum('eni,eih->enh', jax.nn.silu(g) * u, w_down)
        routed = jnp.einsum('enh,ne->nh', y, comb)
        shared = jax.nn.silu(h @ sh_gate) * (h @ sh_up) @ sh_down
        sg = jax.nn.sigmoid(h @ sh_gate_w)
        return (routed + sg * shared).reshape(orig)
    x = x + _L0_xattn_ref(_layernorm(x, axis=-1), itok_BxS_13_99985, ctx_2048, ctx_2048, ctx_2048)
    x = x + _L0_ffn_ref(_layernorm(x, axis=-1), L0_ffn_router_w, L0_ffn_w_gate, L0_ffn_w_up, L0_ffn_w_down, L0_ffn_sh_gate, L0_ffn_sh_up, L0_ffn_sh_down, L0_ffn_sh_gate_w)
    return x

_drawn_inputs = setup_inputs


def setup_inputs(seed=0):
    import zlib

    import numpy as np

    out = dict(_drawn_inputs(seed))
    spreads = {}
    factors = {}
    for name, (base, spread) in spreads.items():
        noise = np.random.default_rng([zlib.crc32(name.encode()), seed]).standard_normal(out[name].shape)
        drawn = base * np.exp(spread * noise) if base else spread * noise
        out[name] = jnp.asarray(drawn.astype(out[name].dtype))
    for name, factor in factors.items():
        out[name] = (out[name] * factor).astype(out[name].dtype)
    return out
```

```python
from contextlib import ExitStack

import concourse.bass as bass
from concourse import mybir

F32 = mybir.dt.float32
F32R = mybir.dt.float32r
BF16 = mybir.dt.bfloat16
I32 = mybir.dt.int32
U32 = mybir.dt.uint32
ALU = mybir.AluOpType
ACT = mybir.ActivationFunctionType
AX = mybir.AxisListType

P = 128
D = 512
KD = D // P
NTOK = 2048
C = NTOK // P
E1, F1 = 4, 512
BOUND1 = 6250
TILES1 = NTOK // P + E1 - 1
E2, F2, TOPK = 16, 352, 4
QUARTERS = 4
TILES2 = NTOK * TOPK // P + E2 - 1
CH1 = [P] * (F1 // P)
CH2 = [P, P, F2 - 2 * P]
WG, WU, WD = 0, KD * F2, 2 * KD * F2
WSET = 2 * KD * F2 + len(CH2) * D
EPS = 1e-5
LN = 4

G_SH0 = TILES1
G_RT = G_SH0 + C
G_SH1 = G_RT + TILES2
G_SH2 = G_SH1 + C
G_SH3 = G_SH2 + C
G_END = G_SH3 + C
FILLS = 10
FILL = 8
COMBINE = G_SH1 + 4


def run_steps(eng, first, end, body):
    pairs = (end - first) // 2
    if pairs > 1:
        with eng.Fori(0, pairs) as j:
            for u in range(2):
                body(first + u + 2 * j, (first + u) // 2 + j, (first + u) % 2)
    elif pairs == 1:
        for u in range(2):
            body(first + u, (first + u) // 2, (first + u) % 2)
    if (end - first) % 2:
        body(end - 1, (end - 1) // 2, (end - 1) % 2)


def build(nc, x, tok, ctx1, router_w, w_gate, w_up, w_down, sh_gate, sh_up, sh_down, sh_gate_w, out):
    x_v = x.rearrange("b s d -> (b s) d").rearrange("(p c) d -> p c d", c=C)
    out_v = out.rearrange("b s d -> (b s) d").rearrange("(p c) d -> p c d", c=C)
    tok_v = tok.rearrange("b s -> (b s)").rearrange("(p c) -> p c", c=C)

    with ExitStack() as ctx:
        def sb(name, shape, dt=F32):
            return ctx.enter_context(nc.sbuf_tensor(name, shape, dt))

        def dram(name, tiles):
            return nc.dram_tensor(name, [tiles * P, D], F32, kind="Internal").ap()

        def sem(name):
            return ctx.enter_context(nc.semaphore(name))

        xs1 = dram("xs1", TILES1)
        y1 = dram("y1", TILES1)
        h2tok = dram("h2tok", C)
        xs2 = dram("xs2", FILLS * FILL)
        y2 = dram("y2", TILES2)

        wset = sb("wset", [P, 2, 2, WSET], F32R)
        raw = sb("raw", [P, WSET])
        x_all = sb("x_all", [P, C, D])
        h_all = sb("h_all", [P, C, D])
        xin = sb("xin", [P, 2, D], F32R)
        hT = sb("hT", [P, 2, 2, KD * P], F32R)
        silu = sb("silu", [P, F1])
        act = sb("act", [P, F1])
        aT = sb("aT", [P, 2, len(CH1) * P], F32R)
        ysb = sb("ysb", [P, 2, D])
        gbuf = sb("gbuf", [P, 8, D])
        rT = gbuf[:, 6:8, :]
        zeros = sb("zeros", [P, D])
        ident = sb("ident", [P, P])
        ident_r = sb("ident_r", [P, P], F32R)
        tri = sb("tri", [P, P], BF16)
        ones = sb("ones", [P, P], BF16)
        tokid = sb("tokid", [P, C], I32)
        wr_rows = sb("wr_rows", [E2 + 1, D])
        wrT = sb("wrT", [P, KD, E2 + 1])
        stats = sb("stats", [P, LN, 6])
        mv = sb("mv", [P, LN, 2])
        var = sb("var", [P, LN])
        std = sb("std", [P, LN])
        rstd = sb("rstd", [P, LN])
        newton = sb("newton", [P, LN])
        logits = sb("logits", [P, C, E2 + 1])
        top8 = sb("top8", [P, C, 8])
        idx8 = sb("idx8", [P, C, 8], U32)
        idxf = sb("idxf", [P, C, TOPK])
        expo = sb("expo", [P, C, E2])
        etop = sb("etop", [P, C, TOPK])
        combw = sb("combw", [P, C, TOPK])
        zsum = sb("zsum", [P, C])
        sgate = sb("sgate", [P, C])
        hot = gbuf[:, 4:6, :].rearrange("p a (b c e) -> p (a b) c e", c=C, e=E2)
        maskb = sb("maskb", [P, C * E2], BF16)
        tot = sb("tot", [P, E2 * C])
        run = sb("run", [P, E2 * C])
        vslot = sb("vslot", [P, C, E2])
        cnt = sb("cnt", [P, E2])
        cexc = sb("cexc", [P, E2])
        padi = sb("padi", [P, E2], I32)
        padf = sb("padf", [P, E2])
        bend = sb("bend", [P, E2])
        slotf = sb("slotf", [P, C, TOPK])
        slot1 = sb("slot1", [P, C], U32)
        slot2 = sb("slot2", [P, C, TOPK], U32)
        iota_e = sb("iota_e", [P, E2])
        iota_t = sb("iota_t", [P, TILES2])
        texp = sb("texp", [P, TILES2])
        iota_w = sb("iota_w", [1, TILES2])
        texi = sb("texi", [P, TILES2], I32)
        tab1 = sb("tab1", [1, TILES1], I32)
        tab_buf = sb("tab_buf", [1, G_END - G_SH0], I32)
        tab_cnt = sb("tab_cnt", [1, G_END - G_SH0], I32)
        tab_free = sb("tab_free", [1, E2], I32)
        cmp_t = gbuf[:, 0:3, :].rearrange("p a d -> p (a d)")[:, 0:TILES2 * E2].rearrange(
            "p (t e) -> p t e", e=E2)

        def bank(name):
            return ctx.enter_context(nc.psum_tensor(name, [P, 512], F32))
        xT_ps, g_ps, u_ps, aT_ps, y_ps, lg_ps, cum_ps, tot_ps = [
            bank(n) for n in ("xT_ps", "g_ps", "u_ps", "aT_ps", "y_ps", "lg_ps", "cum_ps", "tot_ps")]
        ct_banks = [g_ps, u_ps]

        s_const = sem("s_const")
        s_tok = sem("s_tok")
        s_x = [sem(f"s_xq{i}") for i in range(4)]
        s_wr = sem("s_wr")
        s_ctx = [sem(f"s_ctx{i}") for i in range(2)]
        s_zero1 = sem("s_zero1")
        s_zero2 = sem("s_zero2")
        s_ln = sem("s_ln")
        s_var = sem("s_var")
        s_std = sem("s_std")
        s_h1 = sem("s_h1")
        s_dve = sem("s_dve")
        s_mask1 = sem("s_mask1")
        s_mask2 = sem("s_mask2")
        s_cum1 = sem("s_cum1")
        s_cum2 = sem("s_cum2")
        s_slot1 = sem("s_slot1")
        s_slot2 = sem("s_slot2")
        s_scat1 = [sem(f"s_scat1_{c}") for c in range(C)]
        s_scat2 = [sem(f"s_scat2_{c}") for c in range(C)]
        s_ctp = sem("s_ctp")
        s_cth = sem("s_cth")
        s_ctl = sem("s_ctl")
        s_wrp = sem("s_wrp")
        s_wrT = sem("s_wrT")
        s_in = [sem(f"s_in{i}") for i in range(2)]
        s_xT = sem("s_xT")
        s_hhi = sem("s_hhi")
        s_hT = sem("s_hT")
        s_gate = sem("s_gate")
        s_up = sem("s_up")
        s_silu = sem("s_silu")
        s_act = sem("s_act")
        s_aT = sem("s_aT")
        s_ahi = sem("s_ahi")
        s_aTs = sem("s_aTs")
        s_down = sem("s_down")
        s_y = sem("s_y")
        s_yst = [sem(f"s_yst{i}") for i in range(2)]
        s_g1 = [sem(f"s_g1_{i}") for i in range(4)]
        s_x1 = sem("s_x1")
        s_h2 = sem("s_h2")
        s_h2st = sem("s_h2st")
        s_rp = sem("s_rp")
        s_rT = sem("s_rT")
        s_lg = sem("s_lg")
        s_exin = sem("s_exin")
        s_exp = sem("s_exp")
        s_raw = [sem(f"s_raw{i}") for i in range(3)]
        s_split = [sem(f"s_split{i}") for i in range(3)]
        s_whi = sem("s_whi")
        s_pool = sem("s_pool")
        s_gy = [sem(f"s_gy{i}") for i in range(2)]
        s_cmb = sem("s_cmb")
        s_cstep = sem("s_cstep")
        s_out = sem("s_out")
        s_fin = sem("s_fin")

        PIECES = [(WG, KD, F2), (WU, KD, F2), (WD, len(CH2), D)]

        wflat = wset[:].rearrange("p b h w -> p (b h w)")

        def ct(e, part):
            return wset[:, e // 2, part, (e % 2) * KD * F1:(e % 2 + 1) * KD * F1].rearrange(
                "p (k f) -> p k f", k=KD)

        def raw_ctx(e):
            o = (e % 2) * KD * F1
            return raw[:, o:o + KD * F1].rearrange("p (k f) -> p k f", k=KD)

        def tile_of(rows, c):
            if isinstance(c, int):
                return rows[:, c, :]
            return rows[:, bass.ds(c, 1), :].rearrange("p a d -> p (a d)")

        def stored_before(half, par):
            in_layer1 = (TILES1 + 1 - par) // 2
            first = G_RT + (G_RT % 2 != par)
            return in_layer1 + half - first // 2

        with nc.Block() as block:

            @block.sync
            def _(sp):
                def load_set(n, gate, up, down):
                    for i, src in enumerate((gate, up)):
                        off, k, w = PIECES[i]
                        if not (isinstance(n, int) and n == 0):
                            sp.wait_ge(s_split[i], n)
                        sp.dma_start(raw[:, off:off + k * w].rearrange("p (k f) -> p k f", k=k),
                                     src).then_inc(s_raw[i], 16)
                    off = PIECES[2][0]
                    if not (isinstance(n, int) and n == 0):
                        sp.wait_ge(s_split[2], n)
                    sp.dma_start(raw[:, off:off + 2 * D].rearrange("p (k f) -> p k f", k=2),
                                 down[0:2 * P, :].rearrange("(k p) f -> p k f", p=P)).then_inc(s_raw[2], 16)
                    sp.dma_start(raw[0:CH2[2], off + 2 * D:off + 3 * D],
                                 down[2 * P:F2, :]).then_inc(s_raw[2], 16)

                def load_quarter(i, n):
                    cols = slice(i * F2, (i + 1) * F2)
                    load_set(n, sh_gate[:, cols].rearrange("(k p) f -> p k f", p=P),
                             sh_up[:, cols].rearrange("(k p) f -> p k f", p=P), sh_down[cols, :])

                def load_expert(e, n):
                    one = bass.ds(e, 1)
                    load_set(n, w_gate[one].rearrange("e (k p) f -> p (e k) f", p=P),
                             w_up[one].rearrange("e (k p) f -> p (e k) f", p=P),
                             w_down[one].rearrange("e r f -> (e r) f"))

                sp.dma_start(tokid[:], tok_v).then_inc(s_tok, 16)
                for i in range(4):
                    sp.dma_start(x_all[:, 4 * i:4 * i + 4, :], x_v[:, 4 * i:4 * i + 4, :]).then_inc(s_x[i], 16)
                for e in (0, 1):
                    sp.dma_start(raw_ctx(e), ctx1[e].rearrange("(k p) f -> p k f", p=P)).then_inc(s_ctx[0], 16)
                sp.dma_start(wr_rows[0:E2, :], router_w).then_inc(s_wr, 16)
                sp.dma_start(wr_rows[E2:E2 + 1, :], sh_gate_w.rearrange("d o -> o d")).then_inc(s_wr, 16)
                sp.wait_ge(s_const, 1)
                sp.dma_start(xs1.rearrange("(t p) d -> p t d", p=P),
                             zeros[:].unsqueeze(1).to_broadcast([P, TILES1, D])).then_inc(s_zero1, 16)
                sp.wait_ge(s_ctp, 2 * KD)
                for e in (2, 3):
                    sp.dma_start(raw_ctx(e), ctx1[e].rearrange("(k p) f -> p k f", p=P)).then_inc(s_ctx[1], 16)
                sp.wait_ge(s_ctp, E1 * KD)
                load_quarter(0, 0)
                with sp.Fori(0, FILLS) as n:
                    sp.wait_ge(s_down, 1 + (TILES1 - 1) // FILLS * n)
                    sp.dma_start(xs2[bass.ds(n * (FILL * P), FILL * P), :].rearrange("(t p) d -> p t d", p=P),
                                 zeros[:].unsqueeze(1).to_broadcast([P, FILL, D])).then_inc(s_zero2, 16)
                for c in range(C):
                    sp.wait_ge(s_h2, c + 1)
                    sp.dma_start(h2tok[c * P:(c + 1) * P, :], h_all[:, c, :]).then_inc(s_h2st, 16)
                with sp.Fori(0, E2) as e:
                    load_expert(e, e + 1)
                for i in range(1, QUARTERS):
                    load_quarter(i, E2 + i)
                for c in range(C):
                    sp.wait_ge(s_fin, c + 1)
                    sp.dma_start(out_v[:, c, :], x_all[:, c, :]).then_inc(s_out, 16)
                sp.wait_ge(s_out, 16 * C)

            @block.gpsimd
            def _(pool):
                pool.memset(zeros[:], 0.0).then_inc(s_const, 1)
                pool.memset(ident[:], 0.0).then_inc(s_const, 1)
                pool.memset(tri[:], 1.0).then_inc(s_const, 1)
                pool.memset(ones[:], 1.0).then_inc(s_const, 1)
                pool.iota(iota_e[:], [[1, E2]], base=0, channel_multiplier=0,
                          allow_small_or_imprecise_dtypes=True).then_inc(s_const, 1)
                pool.iota(iota_t[:], [[1, TILES2]], base=0, channel_multiplier=0,
                          allow_small_or_imprecise_dtypes=True).then_inc(s_const, 1)
                pool.wait_ge(s_const, 6)
                pool.affine_select(out=ident_r[:], in_=ident[:], compare_op=ALU.not_equal, fill=1.0, base=0,
                                   pattern=[[-1, P]], channel_multiplier=1).then_inc(s_const, 1)
                pool.wait_ge(s_const, 7)
                pool.affine_select(out=ident[:], in_=ident[:], compare_op=ALU.not_equal, fill=1.0, base=0,
                                   pattern=[[-1, P]], channel_multiplier=1).then_inc(s_const, 1)
                pool.affine_select(out=tri[:], in_=tri[:], compare_op=ALU.is_gt, fill=0.0, base=0,
                                   pattern=[[1, P]], channel_multiplier=-1).then_inc(s_const, 1)

                pool.wait_ge(s_zero1, 16)
                pool.wait_ge(s_slot1, 1)
                for c in range(C):
                    pool.wait_ge(s_h1, c + 1)
                    pool.indirect_dma_start(xs1, bass.IndirectOffsetOnAxis(ap=slot1[:, c:c + 1], axis=0),
                                            h_all[:, c, :], None).then_inc(s_scat1[c], 16)

                def piece(buf, i):
                    off, k, w = PIECES[i]
                    return (wset[:, buf, 0, off:off + k * w], wset[:, buf, 1, off:off + k * w],
                            raw[:, off:off + k * w])

                def views(buf, i):
                    hi, lo, r = piece(buf, i)
                    if i < 2:
                        return [(hi, lo, r)]
                    m = CH2[2]
                    return [(hi[:, 0:2 * D], lo[:, 0:2 * D], r[:, 0:2 * D]),
                            (hi[0:m, 2 * D:], lo[0:m, 2 * D:], r[0:m, 2 * D:])]

                def split_piece(buf, i, n, hi_too=True):
                    pool.wait_ge(s_raw[i], 16 * (n + 1) * (1 + (i == 2)))
                    parts = views(buf, i)
                    if hi_too:
                        for hi, lo, r in parts:
                            zero = zeros[0:r.shape[0], 0:1].to_broadcast(list(r.shape))
                            last = pool.tensor_tensor(hi, r, zero, ALU.add)
                        last.then_inc(s_pool, 1)
                        pool.wait_ge(s_pool, 3 * n + i - 2)
                    for m, (hi, lo, r) in enumerate(parts):
                        last = pool.tensor_tensor(lo, r, hi.bitcast(F32), ALU.subtract)
                    last.then_inc(s_split[i], 1)

                for par in range(2):
                    pool.wait_ge(s_yst[par], 16 * ((TILES1 + 1 - par) // 2))
                for c in range(C):
                    if c >= 4:
                        pool.wait_ge(s_x1, c - 3)
                    pool.indirect_dma_start(gbuf[:, c % 4, :], None, y1,
                                            bass.IndirectOffsetOnAxis(ap=slot1[:, c:c + 1], axis=0)
                                            ).then_inc(s_g1[c % 4], 16)
                    if c % 4 == 3 and c < 12:
                        pool.wait_ge(s_whi, c // 4 + 1)
                        split_piece(0, c // 4, 0, hi_too=False)
                pool.wait_ge(s_down, TILES1)
                for i in range(3):
                    split_piece(1, i, 1)

                pool.wait_ge(s_slot2, 1)
                pool.wait_ge(s_zero2, 16 * FILLS)
                for c in range(C):
                    for k in range(TOPK):
                        pool.indirect_dma_start(xs2, bass.IndirectOffsetOnAxis(ap=slot2[:, c, k:k + 1], axis=0),
                                                h_all[:, c, :], None).then_inc(s_scat2[c], 16)
                pool.wait_ge(s_down, G_RT)
                for i in range(3):
                    split_piece(0, i, 2)

                def rest(n, buf, e):
                    pool.wait_ge(s_down, pool.value_load(tab_free[0:1, bass.ds(e, 1)], min_val=G_RT,
                                                         max_val=G_SH1))
                    for i in range(3):
                        split_piece(buf, i, n)
                with pool.Fori(0, 7) as j:
                    rest(3 + 2 * j, 1, 2 * j)
                    rest(4 + 2 * j, 0, 2 * j + 1)
                rest(17, 1, 14)

                for par in range(2):
                    pool.wait_ge(s_yst[par], 16 * stored_before((G_SH1 + (G_SH1 % 2 != par)) // 2, par))
                for c in range(C):
                    if c >= 2:
                        pool.wait_ge(s_cmb, c - 1)
                    for k in range(TOPK):
                        pool.indirect_dma_start(gbuf[:, 4 * (c % 2) + k, :], None, y2,
                                                bass.IndirectOffsetOnAxis(ap=slot2[:, c, k:k + 1], axis=0)
                                                ).then_inc(s_gy[c % 2], 16)
                    if c in (1, 4, 7):
                        if c == 1:
                            pool.wait_ge(s_down, G_SH1)
                        split_piece(0, c // 3, 18)
                pool.wait_ge(s_down, G_SH2)
                for i in range(3):
                    split_piece(1, i, 19)

            @block.scalar
            def _(a):
                def roots(n):
                    a.wait_ge(s_var, n + 1)
                    a.activation(std[:], var[:], ACT.Sqrt).then_inc(s_std, 1)
                for n in range(C // LN):
                    roots(n)

                for e in range(E1):
                    for k in range(KD):
                        n = e * KD + k
                        a.wait_ge(s_ctp, n + 1)
                        a.activation(ct(e, 0)[:, k, :], ct_banks[n % 2][:], ACT.Copy).then_inc(s_cth, 1)
                a.wait_ge(s_wrp, 1)
                a.activation(wrT[:], lg_ps[:, 0:KD * (E2 + 1)].rearrange("p (k e) -> p k e", k=KD),
                             ACT.Copy).then_inc(s_wrT, 1)

                def load_rows(src, tile, par):
                    a.dma_start(xin[:, par, :].bitcast(F32), src[bass.ds(tile * P, P), :]).then_inc(s_in[par], 16)

                def hi_x(g, par):
                    a.wait_ge(s_xT, g + 1)
                    a.activation(hT[:, par, 0, :], xT_ps[:], ACT.Copy).then_inc(s_hhi, 1)

                def hi_a(g, chunks):
                    a.wait_ge(s_aT, g + 1)
                    if chunks[-1] == P:
                        n = len(chunks) * P
                        a.activation(aT[:, 0, 0:n], aT_ps[:, 0:n], ACT.Copy).then_inc(s_ahi, 1)
                    else:
                        m = chunks[-1]
                        a.activation(aT[:, 0, 0:2 * P], aT_ps[:, 0:2 * P], ACT.Copy)
                        a.activation(aT[0:m, 0, 2 * P:3 * P], aT_ps[0:m, 2 * P:3 * P], ACT.Copy).then_inc(s_ahi, 1)

                def do_silu(g, f):
                    a.wait_ge(s_gate, g + 1)
                    if not (isinstance(g, int) and g == 0):
                        a.wait_ge(s_act, g)
                    a.activation(silu[:, 0:f], g_ps[:, 0:f], ACT.Silu).then_inc(s_silu, 1)

                def y_copy(g, par, before):
                    a.wait_ge(s_down, g + 1)
                    if not (isinstance(before, int) and before == 0):
                        a.wait_ge(s_yst[par], 16 * before)
                    a.activation(ysb[:, par, :], y_ps[:], ACT.Copy).then_inc(s_y, 1)

                def y_store(dst, g, tile, par):
                    a.wait_ge(s_y, g + 1)
                    a.dma_start(dst[bass.ds(tile * P, P), :], ysb[:, par, :]).then_inc(s_yst[par], 16)

                for c in range(C):
                    a.wait_ge(s_scat1[c], 16)
                load_rows(xs1, 0, 0)
                load_rows(xs1, 1, 1)
                hi_x(0, 0)
                load_rows(xs1, 2, 0)
                hi_x(1, 1)
                load_rows(xs1, 3, 1)
                do_silu(0, F1)

                def layer1(loads, stores):
                    def body(g, half, par):
                        if stores:
                            y_store(y1, g - 2, g - 2, par)
                        hi_a(g - 1, CH1)
                        hi_x(g + 1, 1 - par)
                        if loads:
                            load_rows(xs1, g + 3, 1 - par)
                        do_silu(g, F1)
                        y_copy(g - 1, 1 - par, half - (1 - par))
                    return body
                last = TILES1 - 1
                layer1(True, False)(1, 0, 1)
                layer1(True, True)(2, 1, 0)
                run_steps(a, 3, last - 2, layer1(True, True))
                run_steps(a, last - 2, last, layer1(False, True))
                y_store(y1, last - 2, last - 2, last % 2)
                hi_a(last - 1, CH1)
                do_silu(last, F1)
                y_copy(last - 1, (last - 1) % 2, (last - 1) // 2)
                y_store(y1, last - 1, last - 1, (last - 1) % 2)
                hi_a(last, CH1)
                y_copy(last, last % 2, last // 2)
                y_store(y1, last, last, last % 2)

                a.wait_ge(s_down, TILES1)
                for i, (off, k, w) in enumerate(PIECES):
                    a.wait_ge(s_raw[i], 16 * (1 + (i == 2)))
                    if i < 2:
                        a.activation(wset[:, 0, 0, off:off + k * w], raw[:, off:off + k * w],
                                     ACT.Copy).then_inc(s_whi, 1)
                    else:
                        a.activation(wset[:, 0, 0, off:off + 2 * D], raw[:, off:off + 2 * D], ACT.Copy)
                        a.activation(wset[0:CH2[2], 0, 0, off + 2 * D:off + 3 * D],
                                     raw[0:CH2[2], off + 2 * D:off + 3 * D], ACT.Copy).then_inc(s_whi, 1)

                for c in range(C):
                    if c % LN == 0:
                        roots((C + c) // LN)
                    a.wait_ge(s_rp, c + 1)
                    if c >= 2:
                        a.wait_ge(s_lg, c - 1)
                    a.activation(rT[:, c % 2, :], xT_ps[:], ACT.Copy).then_inc(s_rT, 1)
                a.wait_ge(s_exin, 1)
                a.activation(expo[:], expo[:], ACT.Exp).then_inc(s_exp, 1)
                a.activation(etop[:], etop[:], ACT.Exp).then_inc(s_exp, 1)
                a.activation(sgate[:], logits[:, :, E2], ACT.Sigmoid).then_inc(s_exp, 1)

                a.wait_ge(s_h2st, 16 * C)
                g = G_SH0
                load_rows(h2tok, 0, g % 2)
                load_rows(h2tok, 1, 1 - g % 2)
                hi_x(g, g % 2)
                load_rows(h2tok, 2, g % 2)
                hi_x(g + 1, 1 - g % 2)
                load_rows(h2tok, 3, 1 - g % 2)
                do_silu(g, F2)

                def layer2(first):
                    copies = G_RT <= first - 1 < G_SH1
                    stores = G_RT <= first - 2 < G_SH1
                    row = first + 3
                    src, base = next(((s, b) for s, b, e in (
                        (h2tok, G_SH0, G_RT), (xs2, G_RT, G_SH1), (h2tok, G_SH1, G_SH2),
                        (h2tok, G_SH2, G_SH3), (h2tok, G_SH3, G_END)) if b <= row < e), (None, 0))
                    if row in (G_RT, G_RT + 1):
                        src = None

                    def body(g, half, par):
                        if stores:
                            y_store(y2, g - 2, g - 2 - G_RT, par)
                        hi_a(g - 1, CH2)
                        hi_x(g + 1, 1 - par)
                        if src is not None:
                            load_rows(src, g + 3 - base, 1 - par)
                        do_silu(g, F2)
                        if copies:
                            y_copy(g - 1, 1 - par, stored_before(half - (1 - par), 1 - par))
                    return body

                cuts = [G_SH0 + 1, G_RT - 3, G_RT - 1, G_RT + 1, G_RT + 2, G_SH1 - 3, G_SH1 + 1, G_SH1 + 2,
                        G_SH2 - 3, G_SH3 - 3, G_END - 3, G_END - 1]
                for first, end in zip(cuts, cuts[1:]):
                    if first == G_RT - 1:
                        for c in range(C):
                            a.wait_ge(s_scat2[c], 16 * TOPK)
                        load_rows(xs2, 0, G_RT % 2)
                        load_rows(xs2, 1, 1 - G_RT % 2)
                    run_steps(a, first, end, layer2(first))
                g = G_END - 1
                hi_a(g - 1, CH2)
                do_silu(g, F2)
                hi_a(g, CH2)

            @block.tensor
            def _(pe):
                pe.wait_ge(s_const, 9)
                def contexts(i):
                    pe.wait_ge(s_ctx[i], 32)
                    for e in (2 * i, 2 * i + 1):
                        for k in range(KD):
                            n = e * KD + k
                            if n >= 2:
                                pe.wait_ge(s_ctl, n - 1)
                            for f in range(KD):
                                last = pe.transpose(ct_banks[n % 2][:, f * P:(f + 1) * P],
                                                    raw_ctx(e)[:, f, k * P:(k + 1) * P], ident[:])
                            last.then_inc(s_ctp, 1)
                def ranks(width, s_mask, s_cum):
                    pe.wait_ge(s_mask, 1)
                    pe.matmul(cum_ps[:, 0:width], tri[:], maskb[:, 0:width], start=True, stop=True)
                    pe.matmul(tot_ps[:, 0:width], ones[:], maskb[:, 0:width], start=True,
                              stop=True).then_inc(s_cum, 1)
                ranks(C * E1, s_mask1, s_cum1)
                contexts(0)
                contexts(1)
                pe.wait_ge(s_wr, 32)
                for k in range(KD):
                    last = pe.transpose(lg_ps[:, k * (E2 + 1):(k + 1) * (E2 + 1)], wr_rows[:, k * P:(k + 1) * P],
                                        ident[0:E2 + 1, 0:E2 + 1])
                last.then_inc(s_wrp, 1)

                def x_transposes(g, half, par):
                    pe.wait_ge(s_in[par], 16 * (half + 1))
                    if not (isinstance(g, int) and g == 0):
                        pe.wait_ge(s_hT, g)
                    for k in range(KD):
                        last = pe.transpose(xT_ps[:, k * P:(k + 1) * P].bitcast(F32R), xin[:, par, k * P:(k + 1) * P],
                                            ident_r[:])
                    last.then_inc(s_xT, 1)

                def a_transposes(g, chunks):
                    pe.wait_ge(s_act, g + 1)
                    for k, m in enumerate(chunks):
                        last = pe.transpose(aT_ps[0:m, k * P:(k + 1) * P], act[:, k * P:k * P + m], ident[:])
                    last.then_inc(s_aT, 1)

                def product(ps, left, right, chunks, done):
                    n = 3 * len(chunks)
                    i = 0
                    for k, m in enumerate(chunks):
                        for l, r in ((0, 0), (0, 1), (1, 0)):
                            mm = pe.matmul(ps, left(l, k, m), right(r, k, m), start=(i == 0), stop=(i == n - 1))
                            i += 1
                    mm.then_inc(done, 1)

                def h_left(par):
                    return lambda l, k, m: hT[0:m, par, l, k * P:(k + 1) * P]

                def a_left(l, k, m):
                    return aT[0:m, l, k * P:(k + 1) * P]

                def context_of(g):
                    at = pe.value_load(tab1[0:1, bass.ds(g, 1)], min_val=0, max_val=2 * WSET + KD * F1)
                    return lambda r, k, m: wflat[:, bass.ds(at + (r * WSET + k * F1), F1)]

                def down1(g, right):
                    pe.wait_ge(s_aTs, g + 1)
                    if not (isinstance(g, int) and g == 0):
                        pe.wait_ge(s_y, g)
                    product(y_ps[:], a_left, right, CH1, s_down)

                def gate1(g, par, right):
                    pe.wait_ge(s_hT, g + 1)
                    product(g_ps[:], h_left(par), right, CH1, s_gate)

                pe.wait_ge(s_ctl, E1 * KD)
                pe.wait_ge(s_slot1, 1)
                x_transposes(0, 0, 0)
                x_transposes(1, 0, 1)
                gate1(0, 0, context_of(0))

                def layer1(g, half, par):
                    own, before = context_of(g), context_of(g - 1)
                    a_transposes(g - 1, CH1)
                    x_transposes(g + 1, half + (1 if par else 0), 1 - par)
                    gate1(g, par, own)
                    down1(g - 1, before)
                layer1(1, 0, 1)
                run_steps(pe, 2, TILES1 - 1, layer1)
                g = TILES1 - 1
                own, before = context_of(g), context_of(g - 1)
                a_transposes(g - 1, CH1)
                gate1(g, g % 2, own)
                down1(g - 1, before)
                a_transposes(g, CH1)
                down1(g, own)

                pe.wait_ge(s_wrT, 1)
                def r_transposes(c):
                    pe.wait_ge(s_h2, c + 1)
                    if c:
                        pe.wait_ge(s_rT, c)
                    for k in range(KD):
                        last = pe.transpose(xT_ps[:, k * P:(k + 1) * P], h_all[:, c, k * P:(k + 1) * P], ident[:])
                    last.then_inc(s_rp, 1)
                def r_logits(c):
                    pe.wait_ge(s_rT, c + 1)
                    for k in range(KD):
                        last = pe.matmul(lg_ps[:, c * (E2 + 1):(c + 1) * (E2 + 1)], rT[:, c % 2, k * P:(k + 1) * P],
                                         wrT[:, k, :], start=(k == 0), stop=(k == KD - 1))
                    last.then_inc(s_lg, 1)
                for c in range(C):
                    r_transposes(c)
                    r_logits(c)

                ranks(C * E2, s_mask2, s_cum2)

                def set_right(at, part):
                    off, _, w = PIECES[part]
                    return lambda r, k, m: wflat[0:m, bass.ds(at + (r * WSET + off + k * w), w)]

                def gate_up(g, par, at, number):
                    pe.wait_ge(s_hT, g + 1)
                    pe.wait_ge(s_split[0], number)
                    product(g_ps[:, 0:F2], h_left(par), set_right(at, 0), [P] * KD, s_gate)
                    pe.wait_ge(s_split[1], number)
                    product(u_ps[:, 0:F2], h_left(par), set_right(at, 1), [P] * KD, s_up)
                    pe.wait_ge(s_split[2], number)

                def down2(g, at):
                    pe.wait_ge(s_aTs, g + 1)
                    pe.wait_ge(s_y, g)
                    product(y_ps[:], a_left, set_right(at, 2), CH2, s_down)

                g = G_SH0
                x_transposes(g, g // 2, g % 2)
                x_transposes(g + 1, (g + 1) // 2, 1 - g % 2)
                gate_up(g, g % 2, 0, 1)

                def quarter0(g, half, par):
                    a_transposes(g - 1, CH2)
                    x_transposes(g + 1, half + (1 if par else 0), 1 - par)
                    gate_up(g, par, 0, 1)
                    down2(g - 1, 0)
                run_steps(pe, G_SH0 + 1, G_RT, quarter0)
                pe.wait_ge(s_slot2, 1)

                def by_table(g, half, par, last=False):
                    row = g - G_SH0
                    at = pe.value_load(tab_buf[0:1, bass.ds(row, 1)], min_val=0, max_val=2 * WSET)
                    number = pe.value_load(tab_cnt[0:1, bass.ds(row, 1)], min_val=1, max_val=E2 + QUARTERS)
                    before = pe.value_load(tab_buf[0:1, bass.ds(row - 1, 1)], min_val=0, max_val=2 * WSET)
                    a_transposes(g - 1, CH2)
                    if not last:
                        x_transposes(g + 1, half + (1 if par else 0), 1 - par)
                    gate_up(g, par, at, number)
                    down2(g - 1, before)
                run_steps(pe, G_RT, G_END - 1, by_table)
                g = G_END - 1
                by_table(g, g // 2, g % 2, last=True)
                a_transposes(g, CH2)
                down2(g, 2 * WSET)

            @block.vector
            def _(v):
                chained = [0]

                def step(ins):
                    chained[0] += 1
                    ins.then_inc(s_dve, 1)
                    v.wait_ge(s_dve, chained[0])

                def normalise(n, c0, done):
                    steps = [7 * n]

                    def link(ins):
                        steps[0] = steps[0] + 1
                        ins.then_inc(s_ln, 1)
                        v.wait_ge(s_ln, steps[0])
                    for i in range(LN):
                        last = v.bn_stats(stats[:, i, :], tile_of(x_all, c0 + i))
                    link(last)
                    for i in range(LN):
                        last = v.bn_aggr(mv[:, i, :], stats[:, i, :])
                    link(last)
                    v.tensor_scalar(var[:], mv[:, :, 1], EPS, None, ALU.add).then_inc(s_var, 1)
                    v.wait_ge(s_std, n + 1)
                    link(v.reciprocal(rstd[:], std[:]))
                    link(v.tensor_tensor(newton[:], rstd[:], rstd[:], ALU.mult))
                    link(v.tensor_tensor(newton[:], newton[:], var[:], ALU.mult))
                    link(v.tensor_scalar(newton[:], newton[:], -0.5, 1.5, ALU.mult, ALU.add))
                    link(v.tensor_tensor(rstd[:], rstd[:], newton[:], ALU.mult))
                    for i in range(LN):
                        v.tensor_scalar(tile_of(h_all, c0 + i), tile_of(x_all, c0 + i), mv[:, i, 0:1],
                                        rstd[:, i:i + 1], ALU.subtract, ALU.mult).then_inc(done, 1)

                def slots(E, tiles, s_cum):
                    W = C * E
                    v.wait_ge(s_cum, 1)
                    tot_e = tot[:, 0:W].rearrange("p (e c) -> p e c", e=E)
                    run_e = run[:, 0:W].rearrange("p (e c) -> p e c", e=E)
                    step(v.tensor_copy(tot_e, tot_ps[:, 0:W].rearrange("p (c e) -> p e c", e=E)))
                    step(v.tensor_reduce(cnt[:, 0:E], tot_e, AX.X, ALU.add))
                    step(v.tensor_scalar(padi[:, 0:E], cnt[:, 0:E], float(P - 1), None, ALU.add))
                    step(v.tensor_scalar(padi[:, 0:E], padi[:, 0:E], 7, 7, ALU.arith_shift_right,
                                         ALU.arith_shift_left))
                    step(v.tensor_copy(padf[:, 0:E], padi[:, 0:E]))
                    step(v.tensor_tensor_scan(bend[:, 0:E], one_row[:, 0:E], padf[:, 0:E], 0.0, ALU.mult, ALU.add))
                    step(v.tensor_tensor_scan(cexc[:, 0:E], one_row[:, 0:E], cnt[:, 0:E], 0.0, ALU.mult, ALU.add))
                    step(v.tensor_tensor(cexc[:, 0:E], bend[:, 0:E], cexc[:, 0:E], ALU.subtract))
                    step(v.tensor_tensor(cexc[:, 0:E], cexc[:, 0:E], padf[:, 0:E], ALU.subtract))
                    step(v.tensor_tensor(cexc[:, 0:E], cexc[:, 0:E], cnt[:, 0:E], ALU.add))
                    step(v.tensor_tensor_scan(run[:, 0:W], one_row[:, 0:W], tot[:, 0:W], 0.0, ALU.mult, ALU.add))
                    step(v.tensor_tensor(run[:, 0:W], run[:, 0:W], tot[:, 0:W], ALU.subtract))
                    step(v.tensor_tensor(run_e, run_e, cexc[:, 0:E].unsqueeze(2).to_broadcast([P, E, C]), ALU.add))
                    step(v.tensor_tensor(vslot[:, :, 0:E], cum_ps[:, 0:W].rearrange("p (c e) -> p c e", e=E),
                                         run[:, 0:W].rearrange("p (e c) -> p c e", e=E), ALU.add))
                    step(v.tensor_scalar(bend[:, 0:E], bend[:, 0:E], 1.0 / P, None, ALU.mult))
                    step(v.tensor_tensor(cmp_t[:, 0:tiles, 0:E],
                                         bend[:, 0:E].unsqueeze(1).to_broadcast([P, tiles, E]),
                                         iota_t[:, 0:tiles].unsqueeze(2).to_broadcast([P, tiles, E]), ALU.is_le))
                    step(v.tensor_reduce(texp[:, 0:tiles], cmp_t[:, 0:tiles, 0:E], AX.X, ALU.add))
                    step(v.tensor_scalar(texp[:, 0:tiles], texp[:, 0:tiles], float(E - 1), None, ALU.min))

                one_row = expo[:].rearrange("p c e -> p (c e)")
                step(v.memset(one_row, 1.0))

                v.wait_ge(s_tok, 16)
                hot1 = hot[:, 0, :, 0:E1]
                ge = hot[:, 1, :, 0:E1 + 1]
                step(v.memset(ge[:, :, 0], 1.0))
                step(v.memset(ge[:, :, E1], 0.0))
                for e in range(1, E1):
                    step(v.tensor_scalar(ge[:, :, e], tokid[:], float(BOUND1 * e), None, ALU.is_ge))
                step(v.tensor_tensor(hot1, ge[:, :, 0:E1], ge[:, :, 1:E1 + 1], ALU.subtract))
                v.tensor_copy(maskb[:, 0:C * E1].rearrange("p (c e) -> p c e", e=E1), hot1).then_inc(s_mask1, 1)
                v.wait_ge(s_const, 9)
                slots(E1, TILES1, s_cum1)
                late = iota_w[0:1, 0:TILES1]
                step(v.tensor_scalar(late, texp[0:1, 0:TILES1], 2.0, float(2 * WSET - 2 * KD * F1), ALU.is_ge,
                                     ALU.mult))
                step(v.scalar_tensor_tensor(out=tab1[:], in0=texp[0:1, 0:TILES1], scalar=float(KD * F1), in1=late,
                                            op0=ALU.mult, op1=ALU.add))
                step(v.tensor_tensor(vslot[:, :, 0:E1], vslot[:, :, 0:E1], hot1, ALU.mult))
                step(v.tensor_reduce(slotf[:, :, 0], vslot[:, :, 0:E1], AX.X, ALU.add))
                v.tensor_copy(slot1[:], slotf[:, :, 0]).then_inc(s_slot1, 1)

                for i in range(C // LN):
                    v.wait_ge(s_x[i], 16)
                    normalise(i, LN * i, s_h1)

                for e in range(E1):
                    for k in range(KD):
                        n = e * KD + k
                        v.wait_ge(s_cth, n + 1)
                        v.tensor_tensor(ct(e, 1)[:, k, :], ct_banks[n % 2][:], ct(e, 0)[:, k, :].bitcast(F32),
                                        ALU.subtract).then_inc(s_ctl, 1)

                def lo_x(g, par):
                    v.wait_ge(s_hhi, g + 1)
                    v.tensor_tensor(hT[:, par, 1, :], xT_ps[:], hT[:, par, 0, :].bitcast(F32),
                                    ALU.subtract).then_inc(s_hT, 1)

                def lo_a(g, chunks):
                    v.wait_ge(s_ahi, g + 1)
                    if chunks[-1] == P:
                        n = len(chunks) * P
                        v.tensor_tensor(aT[:, 1, 0:n], aT_ps[:, 0:n], aT[:, 0, 0:n].bitcast(F32),
                                        ALU.subtract).then_inc(s_aTs, 1)
                    else:
                        m = chunks[-1]
                        v.tensor_tensor(aT[:, 1, 0:2 * P], aT_ps[:, 0:2 * P], aT[:, 0, 0:2 * P].bitcast(F32),
                                        ALU.subtract)
                        v.tensor_tensor(aT[0:m, 1, 2 * P:3 * P], aT_ps[0:m, 2 * P:3 * P],
                                        aT[0:m, 0, 2 * P:3 * P].bitcast(F32), ALU.subtract).then_inc(s_aTs, 1)

                def act1(g):
                    v.wait_ge(s_silu, g + 1)
                    v.tensor_tensor(act[:], g_ps[:], silu[:], ALU.mult).then_inc(s_act, 1)

                def act2(g):
                    v.wait_ge(s_silu, g + 1)
                    v.wait_ge(s_up, g + 1 - TILES1)
                    v.tensor_tensor(act[:, 0:F2], u_ps[:, 0:F2], silu[:, 0:F2], ALU.mult).then_inc(s_act, 1)

                lo_x(0, 0)
                lo_x(1, 1)
                act1(0)

                def layer1(g, half, par):
                    lo_a(g - 1, CH1)
                    lo_x(g + 1, 1 - par)
                    act1(g)
                run_steps(v, 1, TILES1 - 1, layer1)
                g = TILES1 - 1
                lo_a(g - 1, CH1)
                act1(g)
                lo_a(g, CH1)

                for turn in range(C // LN):
                    for i in range(LN):
                        v.wait_ge(s_g1[i], 16 * (turn + 1))
                        row = tile_of(x_all, LN * turn + i)
                        v.tensor_tensor(row, row, gbuf[:, i, :], ALU.add).then_inc(s_x1, 1)
                    v.wait_ge(s_x1, LN * (turn + 1))
                    normalise(turn + C // LN, LN * turn, s_h2)

                v.wait_ge(s_lg, C)
                step(v.tensor_copy(logits[:], lg_ps[:, 0:C * (E2 + 1)].rearrange("p (c e) -> p c e", c=C)))
                for c in range(C):
                    last = v.max(top8[:, c, :], logits[:, c, 0:E2])
                step(last)
                for c in range(C):
                    last = v.max_index(idx8[:, c, :], top8[:, c, :], logits[:, c, 0:E2])
                step(last)
                step(v.tensor_copy(idxf[:], idx8[:, :, 0:TOPK]))
                for k in range(TOPK):
                    last = v.tensor_tensor(hot[:, k], iota_e[:].unsqueeze(1).to_broadcast([P, C, E2]),
                                           idxf[:, :, k:k + 1].to_broadcast([P, C, E2]), ALU.is_equal)
                step(last)
                step(v.tensor_tensor(vslot[:], hot[:, 0], hot[:, 1], ALU.add))
                step(v.tensor_tensor(vslot[:], vslot[:], hot[:, 2], ALU.add))
                v.tensor_tensor(maskb[:].rearrange("p (c e) -> p c e", e=E2), vslot[:], hot[:, 3],
                                ALU.add).then_inc(s_mask2, 1)
                slots(E2, TILES2, s_cum2)
                one_hot_sum = run[:].rearrange("p (c e) -> p c e", e=E2)
                for k in range(TOPK):
                    step(v.tensor_tensor(one_hot_sum, hot[:, k], vslot[:], ALU.mult))
                    step(v.tensor_reduce(slotf[:, :, k], one_hot_sum, AX.X, ALU.add))
                step(v.tensor_copy(slot2[:], slotf[:]))
                rt = G_RT - G_SH0
                step(v.memset(tab_buf[:, 0:rt], 0))
                step(v.memset(tab_cnt[:, 0:rt], 1))
                step(v.tensor_scalar(tab_cnt[:, rt:rt + TILES2], texp[0:1, :], 2.0, None, ALU.add))
                step(v.tensor_scalar(texi[0:1, :], texp[0:1, :], 1.0, None, ALU.add))
                step(v.tensor_scalar(texi[0:1, :], texi[0:1, :], 1, None, ALU.bitwise_and))
                step(v.tensor_scalar(tab_buf[:, rt:rt + TILES2], texi[0:1, :], float(2 * WSET), None, ALU.mult))
                for i in range(1, QUARTERS):
                    a0 = G_SH1 - G_SH0 + (i - 1) * C
                    step(v.memset(tab_buf[:, a0:a0 + C], i % 2 * 2 * WSET))
                    step(v.memset(tab_cnt[:, a0:a0 + C], E2 + 1 + i))
                v.tensor_scalar(tab_free[:], bend[0:1, :], float(G_RT), None, ALU.add).then_inc(s_slot2, 1)

                top = top8[:, :, 0:TOPK]
                first = top8[:, :, 0:1]
                step(v.tensor_tensor(etop[:], top, first.to_broadcast([P, C, TOPK]), ALU.subtract))
                v.tensor_tensor(expo[:], logits[:, :, 0:E2], first.to_broadcast([P, C, E2]),
                                ALU.subtract).then_inc(s_exin, 1)
                v.wait_ge(s_exp, 3)
                step(v.tensor_reduce(zsum[:], expo[:], AX.X, ALU.add))
                step(v.reciprocal(zsum[:], zsum[:]))
                step(v.tensor_tensor(etop[:], etop[:], zsum[:].unsqueeze(2).to_broadcast([P, C, TOPK]), ALU.mult))
                step(v.tensor_reduce(zsum[:], etop[:], AX.X, ALU.add))
                step(v.tensor_scalar(zsum[:], zsum[:], 1e-9, None, ALU.max))
                step(v.reciprocal(zsum[:], zsum[:]))
                step(v.tensor_tensor(combw[:], etop[:], zsum[:].unsqueeze(2).to_broadcast([P, C, TOPK]), ALU.mult))

                def add_y(g, c):
                    v.wait_ge(s_down, g + 1)
                    v.tensor_tensor(tile_of(h_all, c), y_ps[:], tile_of(h_all, c), ALU.add).then_inc(s_y, 1)

                def halves(g, par):
                    lo_a(g - 1, CH2)
                    lo_x(g + 1, 1 - par)
                    act2(g)

                g = G_SH0
                lo_x(g, g % 2)
                lo_x(g + 1, 1 - g % 2)
                act2(g)
                for g in range(G_SH0 + 1, G_RT + 1):
                    halves(g, g % 2)
                    c = g - 1 - G_SH0
                    v.wait_ge(s_scat2[c], 16 * TOPK)
                    v.wait_ge(s_h2st, 16 * C)
                    v.wait_ge(s_down, g)
                    v.tensor_copy(tile_of(h_all, c), y_ps[:]).then_inc(s_y, 1)
                run_steps(v, G_RT + 1, G_SH1 + 1, lambda g, half, par: halves(g, par))

                def combine(c, par, turn):
                    v.wait_ge(s_gy[par], 16 * TOPK * (turn + 1))
                    row = tile_of(x_all, c)
                    for k in range(TOPK):
                        if k:
                            v.wait_ge(s_cstep, 3 * c + k)
                        ins = v.scalar_tensor_tensor(
                            out=row, in0=gbuf[:, 4 * par + k, :],
                            scalar=combw[:, bass.ds(c, 1), k:k + 1].rearrange("p a k -> p (a k)"),
                            in1=row, op0=ALU.mult, op1=ALU.add)
                        ins.then_inc(s_cmb if k == TOPK - 1 else s_cstep, 1)

                def with_sum(c0):
                    def body(g, half, par):
                        halves(g, par)
                        add_y(g - 1, g - c0)
                    return body

                run_steps(v, G_SH1 + 1, COMBINE, with_sum(G_SH1 + 1))
                off = COMBINE - G_SH1 - 1
                with v.Fori(0, (C - off) // 2) as j:
                    for u in range(2):
                        g = COMBINE + u + 2 * j
                        halves(g, (COMBINE + u) % 2)
                        add_y(g - 1, off + u + 2 * j)
                        combine(2 * j + u, u, j)
                n = (C - off) // 2 * 2
                for i in range(n, C):
                    g = COMBINE + i
                    halves(g, g % 2)
                    add_y(g - 1, (off + i) % C)
                    combine(i, i % 2, i // 2)
                g0 = COMBINE + C
                run_steps(v, g0, G_SH3 + 1, with_sum(G_SH2 + 1))

                def last_sum(g, c):
                    v.wait_ge(s_down, g + 1)
                    v.tensor_tensor(tile_of(h_all, c), y_ps[:], tile_of(h_all, c), ALU.add).then_inc(s_y, 1)
                    v.wait_ge(s_y, g + 1)
                    gate = sgate[:, c:c + 1] if isinstance(c, int) else sgate[:, bass.ds(c, 1)]
                    row = tile_of(x_all, c)
                    v.scalar_tensor_tensor(out=row, in0=tile_of(h_all, c), scalar=gate, in1=row, op0=ALU.mult,
                                           op1=ALU.add).then_inc(s_fin, 1)

                def final(g, half, par):
                    halves(g, par)
                    last_sum(g - 1, g - 1 - G_SH3)
                run_steps(v, G_SH3 + 1, G_END - 1, final)
                g = G_END - 1
                lo_a(g - 1, CH2)
                act2(g)
                last_sum(g - 1, C - 2)
                lo_a(g, CH2)
                last_sum(g, C - 1)


_INS = ["x", "itok_BxS_13_99985", "ctx_2048", "L0_ffn_router_w", "L0_ffn_w_gate", "L0_ffn_w_up", "L0_ffn_w_down",
        "L0_ffn_sh_gate", "L0_ffn_sh_up", "L0_ffn_sh_down", "L0_ffn_sh_gate_w"]

_OUTS = [((4, 512, 512), "float32")]


def kernel(**inputs):
    import numpy as _np
    import concourse.bacc as _bacc
    from concourse import mybir as _mybir
    from concourse.bass_utils import run_bass_kernel_spmd as _run

    nc = _bacc.Bacc("TRN2", target_bir_lowering=False, num_devices=1)
    arrays, args = {}, []
    for name in _INS:
        a = _np.ascontiguousarray(inputs[name])
        arrays[f"in_{name}_dram"] = a
        args.append(nc.dram_tensor(f"in_{name}_dram", a.shape, _mybir.dt.from_np(a.dtype), kind="ExternalInput").ap())
    for i, (shape, dtype) in enumerate(_OUTS):
        dt = _mybir.dt.from_np(_np.dtype(dtype))
        args.append(nc.dram_tensor(f"out_{i}_dram", shape, dt, kind="ExternalOutput").ap())
    build(nc, *args)
    r = _run(nc, [arrays], core_ids=[0])
    return r.results[0]["out_0_dram"]
```

```python
from contextlib import ExitStack

import concourse.bass as bass
from concourse import mybir

F32 = mybir.dt.float32
F32R = mybir.dt.float32r
BF16 = mybir.dt.bfloat16
I32 = mybir.dt.int32
U32 = mybir.dt.uint32
ALU = mybir.AluOpType
ACT = mybir.ActivationFunctionType
AX = mybir.AxisListType

P = 128
D = 512
KD = D // P
NTOK = 2048
C = NTOK // P
E1, F1 = 4, 512
BOUND1 = 6250
TILES1 = NTOK // P + E1 - 1
E2, F2, TOPK = 16, 352, 4
QUARTERS = 4
TILES2 = NTOK * TOPK // P + E2 - 1
CH1 = [P] * (F1 // P)
CH2 = [P, P, F2 - 2 * P]
WG, WU, WD = 0, KD * F2, 2 * KD * F2
WSET = 2 * KD * F2 + len(CH2) * D
EPS = 1e-5
LN = 4

G_SH0 = TILES1
G_SH1 = G_SH0 + C
G_RT = G_SH1 + C
G_SH2 = G_RT + TILES2
G_SH3 = G_SH2 + C
G_END = G_SH3 + C
SET_E = 2
SET_SH2 = SET_E + E2
EL = 18
RING = 8
FILLS = 10
FILL = 8
SHARES = G_SH1 + 5
COMBINE = G_SH2 + 3


def run_steps(eng, first, end, body):
    pairs = (end - first) // 2
    if pairs > 1:
        with eng.Fori(0, pairs) as j:
            for u in range(2):
                body(first + u + 2 * j, (first + u) // 2 + j, (first + u) % 2)
    elif pairs == 1:
        for u in range(2):
            body(first + u, (first + u) // 2, (first + u) % 2)
    if (end - first) % 2:
        body(end - 1, (end - 1) // 2, (end - 1) % 2)


def build(nc, x, tok, ctx1, router_w, w_gate, w_up, w_down, sh_gate, sh_up, sh_down, sh_gate_w, out):
    x_v = x.rearrange("b s d -> (b s) d").rearrange("(p c) d -> p c d", c=C)
    out_v = out.rearrange("b s d -> (b s) d").rearrange("(p c) d -> p c d", c=C)
    tok_v = tok.rearrange("b s -> (b s)").rearrange("(p c) -> p c", c=C)

    with ExitStack() as ctx:
        def sb(name, shape, dt=F32):
            return ctx.enter_context(nc.sbuf_tensor(name, shape, dt))

        def dram(name, tiles):
            return nc.dram_tensor(name, [tiles * P, D], F32, kind="Internal").ap()

        def sem(name):
            return ctx.enter_context(nc.semaphore(name))

        xs1 = dram("xs1", TILES1)
        y1 = dram("y1", TILES1)
        h2tok = dram("h2tok", C)
        xs2 = dram("xs2", FILLS * FILL)
        y2 = dram("y2", TILES2)

        wset = sb("wset", [P, 2, 2, WSET], F32R)
        raw = sb("raw", [P, WSET])
        x_all = sb("x_all", [P, C, D])
        h_all = sb("h_all", [P, C, D])
        xin = sb("xin", [P, 2, D], F32R)
        hT = sb("hT", [P, 2, 2, KD * P], F32R)
        silu = sb("silu", [P, F1])
        act = sb("act", [P, F1])
        aT = sb("aT", [P, 2, len(CH1) * P], F32R)
        ysb = sb("ysb", [P, 2, D])
        gbuf = sb("gbuf", [P, RING, D])
        zeros = sb("zeros", [P, D])
        ident = sb("ident", [P, P])
        ident_r = sb("ident_r", [P, P], F32R)
        tri = sb("tri", [P, P], BF16)
        ones = sb("ones", [P, P], BF16)
        tokid = sb("tokid", [P, C], I32)
        wr_rows = sb("wr_rows", [EL, D])
        wrT = sb("wrT", [P, 2, KD, EL], F32R)
        stats = sb("stats", [P, LN, 6])
        mv = sb("mv", [P, LN, 2])
        var = sb("var", [P, LN])
        std = sb("std", [P, LN])
        rstd = sb("rstd", [P, LN])
        newton = sb("newton", [P, LN])
        logits = sb("logits", [P, C, EL])
        top8 = sb("top8", [P, C, 8])
        idx8 = sb("idx8", [P, C, 8], U32)
        idxf = sb("idxf", [P, C, TOPK])
        expo = sb("expo", [P, C, E2])
        etop = sb("etop", [P, C, TOPK])
        combw = sb("combw", [P, C, TOPK])
        zsum = sb("zsum", [P, C])
        sgate = sb("sgate", [P, C])
        hot = gbuf[:, 4:6, :].rearrange("p a (b c e) -> p (a b) c e", c=C, e=E2)
        maskb = sb("maskb", [P, C * E2], BF16)
        tot = sb("tot", [P, E2 * C])
        run = sb("run", [P, E2 * C])
        vslot = sb("vslot", [P, C, E2])
        cnt = sb("cnt", [P, E2])
        cexc = sb("cexc", [P, E2])
        padi = sb("padi", [P, E2], I32)
        padf = sb("padf", [P, E2])
        bend = sb("bend", [P, E2])
        slotf = sb("slotf", [P, C, TOPK])
        slot1 = sb("slot1", [P, C], U32)
        slot2 = sb("slot2", [P, C, TOPK], U32)
        iota_e = sb("iota_e", [P, E2])
        iota_t = sb("iota_t", [P, TILES2])
        texp = sb("texp", [P, TILES2])
        late = sb("late", [1, TILES1])
        texi = sb("texi", [P, TILES2], I32)
        tab1 = sb("tab1", [1, TILES1], I32)
        tab_buf = sb("tab_buf", [1, 1 + G_END - G_RT], I32)
        tab_cnt = sb("tab_cnt", [1, G_END - G_RT], I32)
        tab_free = sb("tab_free", [1, E2], I32)
        tab_ct = sb("tab_ct", [1, 1], I32)
        cmp_t = gbuf[:, 0:3, :].rearrange("p a d -> p (a d)")[:, 0:TILES2 * E2].rearrange(
            "p (t e) -> p t e", e=E2)

        def bank(name):
            return ctx.enter_context(nc.psum_tensor(name, [P, 512], F32))
        xT_ps, g_ps, u_ps, aT_ps, y_ps, lg_ps, cum_ps, tot_ps = [
            bank(n) for n in ("xT_ps", "g_ps", "u_ps", "aT_ps", "y_ps", "lg_ps", "cum_ps", "tot_ps")]
        ct_banks = [g_ps, u_ps]
        lg_banks = [lg_ps, cum_ps]

        s_const = sem("s_const")
        s_tok = sem("s_tok")
        s_x = [sem(f"s_xq{i}") for i in range(4)]
        s_wr = sem("s_wr")
        s_ctx = [sem(f"s_ctx{i}") for i in range(2)]
        s_zero1 = sem("s_zero1")
        s_zero2 = sem("s_zero2")
        s_ln = sem("s_ln")
        s_var = sem("s_var")
        s_std = sem("s_std")
        s_h1 = sem("s_h1")
        s_dve = sem("s_dve")
        s_mask1 = sem("s_mask1")
        s_mask2 = sem("s_mask2")
        s_cum1 = sem("s_cum1")
        s_cum2 = sem("s_cum2")
        s_slot1 = sem("s_slot1")
        s_slot2 = sem("s_slot2")
        s_scat1 = [sem(f"s_scat1_{c}") for c in range(C)]
        s_scat2 = [sem(f"s_scat2_{c}") for c in range(C)]
        s_ctp = sem("s_ctp")
        s_cth = sem("s_cth")
        s_ctl = sem("s_ctl")
        s_wrz = sem("s_wrz")
        s_wrp = sem("s_wrp")
        s_wrhi = sem("s_wrhi")
        s_wrT = sem("s_wrT")
        s_in = [sem(f"s_in{i}") for i in range(2)]
        s_xT = sem("s_xT")
        s_hhi = sem("s_hhi")
        s_hT = sem("s_hT")
        s_gate = sem("s_gate")
        s_up = sem("s_up")
        s_silu = sem("s_silu")
        s_act = sem("s_act")
        s_aT = sem("s_aT")
        s_ahi = sem("s_ahi")
        s_aTs = sem("s_aTs")
        s_down = sem("s_down")
        s_y = sem("s_y")
        s_yst = [sem(f"s_yst{i}") for i in range(2)]
        s_g1 = [sem(f"s_g1_{i}") for i in range(RING)]
        s_x1 = sem("s_x1")
        s_h2 = sem("s_h2")
        s_h2st = [sem(f"s_h2st{j}") for j in range(C // 2)]
        s_row2 = [sem(f"s_row2_{i}") for i in range(RING)]
        s_lg = sem("s_lg")
        s_lgs = sem("s_lgs")
        s_top = sem("s_top")
        s_exin = sem("s_exin")
        s_exp = sem("s_exp")
        s_raw = [sem(f"s_raw{i}") for i in range(3)]
        s_split = [sem(f"s_split{i}") for i in range(3)]
        s_pool = sem("s_pool")
        s_gy = [sem(f"s_gy{i}") for i in range(2)]
        s_cmb = sem("s_cmb")
        s_cstep = sem("s_cstep")
        s_out = sem("s_out")
        s_fin = sem("s_fin")

        PIECES = [(WG, KD, F2), (WU, KD, F2), (WD, len(CH2), D)]

        wflat = wset[:].rearrange("p b h w -> p (b h w)")

        def ct(e, part):
            return wset[:, e // 2, part, (e % 2) * KD * F1:(e % 2 + 1) * KD * F1].rearrange(
                "p (k f) -> p k f", k=KD)

        def raw_ctx(e):
            o = (e % 2) * KD * F1
            return raw[:, o:o + KD * F1].rearrange("p (k f) -> p k f", k=KD)

        def tile_of(rows, c):
            if isinstance(c, int):
                return rows[:, c, :]
            return rows[:, bass.ds(c, 1), :].rearrange("p a d -> p (a d)")

        def stored_before(half, par):
            in_layer1 = (TILES1 + 1 - par) // 2
            first = G_RT + (G_RT % 2 != par)
            return in_layer1 + half - first // 2

        with nc.Block() as block:

            @block.sync
            def _(sp):
                def load_set(n, gate, up, down):
                    for i, src in enumerate((gate, up)):
                        off, k, w = PIECES[i]
                        if not (isinstance(n, int) and n == 0):
                            sp.wait_ge(s_split[i], n)
                        sp.dma_start(raw[:, off:off + k * w].rearrange("p (k f) -> p k f", k=k),
                                     src).then_inc(s_raw[i], 16)
                    off = PIECES[2][0]
                    if not (isinstance(n, int) and n == 0):
                        sp.wait_ge(s_split[2], n)
                    sp.dma_start(raw[:, off:off + 2 * D].rearrange("p (k f) -> p k f", k=2),
                                 down[0:2 * P, :].rearrange("(k p) f -> p k f", p=P)).then_inc(s_raw[2], 16)
                    sp.dma_start(raw[0:CH2[2], off + 2 * D:off + 3 * D],
                                 down[2 * P:F2, :]).then_inc(s_raw[2], 16)

                def load_quarter(i, n):
                    cols = slice(i * F2, (i + 1) * F2)
                    load_set(n, sh_gate[:, cols].rearrange("(k p) f -> p k f", p=P),
                             sh_up[:, cols].rearrange("(k p) f -> p k f", p=P), sh_down[cols, :])

                def load_expert(e, n):
                    one = slice(e, e + 1) if isinstance(e, int) else bass.ds(e, 1)
                    load_set(n, w_gate[one].rearrange("e (k p) f -> p (e k) f", p=P),
                             w_up[one].rearrange("e (k p) f -> p (e k) f", p=P),
                             w_down[one].rearrange("e r f -> (e r) f"))

                sp.dma_start(tokid[:], tok_v).then_inc(s_tok, 16)
                for i in range(4):
                    sp.dma_start(x_all[:, 4 * i:4 * i + 4, :], x_v[:, 4 * i:4 * i + 4, :]).then_inc(s_x[i], 16)
                for e in (0, 1):
                    sp.dma_start(raw_ctx(e), ctx1[e].rearrange("(k p) f -> p k f", p=P)).then_inc(s_ctx[0], 16)
                sp.wait_ge(s_wrz, 1)
                sp.dma_start(wr_rows[0:E2, :], router_w).then_inc(s_wr, 16)
                sp.dma_start(wr_rows[E2:E2 + 1, :], sh_gate_w.rearrange("d o -> o d")).then_inc(s_wr, 16)
                sp.wait_ge(s_const, 1)
                sp.dma_start(xs1.rearrange("(t p) d -> p t d", p=P),
                             zeros[:].unsqueeze(1).to_broadcast([P, TILES1, D])).then_inc(s_zero1, 16)
                sp.wait_ge(s_ctp, 2 * KD)
                for e in (2, 3):
                    sp.dma_start(raw_ctx(e), ctx1[e].rearrange("(k p) f -> p k f", p=P)).then_inc(s_ctx[1], 16)
                sp.wait_ge(s_ctp, E1 * KD)
                load_quarter(0, 0)
                with sp.Fori(0, FILLS) as n:
                    sp.wait_ge(s_down, 1 + (TILES1 - 1) // FILLS * n)
                    sp.dma_start(xs2[bass.ds(n * (FILL * P), FILL * P), :].rearrange("(t p) d -> p t d", p=P),
                                 zeros[:].unsqueeze(1).to_broadcast([P, FILL, D])).then_inc(s_zero2, 16)
                load_quarter(1, 1)
                for c in range(C):
                    sp.wait_ge(s_h2, c + 1)
                    sp.dma_start(h2tok[c * P:(c + 1) * P, :], h_all[:, c, :]).then_inc(s_h2st[c // 2], 16)
                    if c == C - 5:
                        load_expert(0, SET_E)
                def row_back(c):
                    sp.dma_start(gbuf[:, c % RING, :], h2tok[c * P:(c + 1) * P, :]).then_inc(s_row2[c % RING], 16)
                for j in range(C // 2):
                    sp.wait_ge(s_h2st[j], 32)
                sp.wait_ge(s_slot2, 1)
                for c in range(RING):
                    row_back(c)
                load_expert(1, SET_E + 1)
                for c in range(RING, C):
                    sp.wait_ge(s_scat2[c - RING], 16 * TOPK)
                    row_back(c)
                with sp.Fori(0, E2 - 2) as j:
                    load_expert(j + 2, j + SET_E + 2)
                for i in range(2, QUARTERS):
                    load_quarter(i, SET_SH2 + i - 2)
                for c in range(C):
                    sp.wait_ge(s_fin, c + 1)
                    sp.dma_start(out_v[:, c, :], x_all[:, c, :]).then_inc(s_out, 16)
                sp.wait_ge(s_out, 16 * C)

            @block.gpsimd
            def _(pool):
                pool.memset(zeros[:], 0.0).then_inc(s_const, 1)
                pool.memset(wr_rows[:], 0.0).then_inc(s_wrz, 1)
                pool.memset(ident[:], 0.0).then_inc(s_const, 1)
                pool.memset(tri[:], 1.0).then_inc(s_const, 1)
                pool.memset(ones[:], 1.0).then_inc(s_const, 1)
                pool.iota(iota_e[:], [[1, E2]], base=0, channel_multiplier=0,
                          allow_small_or_imprecise_dtypes=True).then_inc(s_const, 1)
                pool.iota(iota_t[:], [[1, TILES2]], base=0, channel_multiplier=0,
                          allow_small_or_imprecise_dtypes=True).then_inc(s_const, 1)
                pool.wait_ge(s_const, 6)
                pool.affine_select(out=ident_r[:], in_=ident[:], compare_op=ALU.not_equal, fill=1.0, base=0,
                                   pattern=[[-1, P]], channel_multiplier=1).then_inc(s_const, 1)
                pool.wait_ge(s_const, 7)
                pool.affine_select(out=ident[:], in_=ident[:], compare_op=ALU.not_equal, fill=1.0, base=0,
                                   pattern=[[-1, P]], channel_multiplier=1).then_inc(s_const, 1)
                pool.affine_select(out=tri[:], in_=tri[:], compare_op=ALU.is_gt, fill=0.0, base=0,
                                   pattern=[[1, P]], channel_multiplier=-1).then_inc(s_const, 1)

                pool.wait_ge(s_zero1, 16)
                pool.wait_ge(s_slot1, 1)
                for c in range(C):
                    pool.wait_ge(s_h1, c + 1)
                    pool.indirect_dma_start(xs1, bass.IndirectOffsetOnAxis(ap=slot1[:, c:c + 1], axis=0),
                                            h_all[:, c, :], None).then_inc(s_scat1[c], 16)

                def piece(buf, i):
                    off, k, w = PIECES[i]
                    return (wset[:, buf, 0, off:off + k * w], wset[:, buf, 1, off:off + k * w],
                            raw[:, off:off + k * w])

                def views(buf, i):
                    hi, lo, r = piece(buf, i)
                    if i < 2:
                        return [(hi, lo, r)]
                    m = CH2[2]
                    return [(hi[:, 0:2 * D], lo[:, 0:2 * D], r[:, 0:2 * D]),
                            (hi[0:m, 2 * D:], lo[0:m, 2 * D:], r[0:m, 2 * D:])]

                def split_piece(buf, i, n):
                    pool.wait_ge(s_raw[i], 16 * (n + 1) * (1 + (i == 2)))
                    parts = views(buf, i)
                    for hi, lo, r in parts:
                        zero = zeros[0:r.shape[0], 0:1].to_broadcast(list(r.shape))
                        last = pool.tensor_tensor(hi, r, zero, ALU.add)
                    last.then_inc(s_pool, 1)
                    pool.wait_ge(s_pool, 3 * n + i + 1)
                    for hi, lo, r in parts:
                        last = pool.tensor_tensor(lo, r, hi.bitcast(F32), ALU.subtract)
                    last.then_inc(s_split[i], 1)

                pool.wait_ge(s_down, pool.value_load(tab_ct[0:1, 0:1], min_val=1, max_val=TILES1))
                for i in range(3):
                    split_piece(0, i, 0)

                for par in range(2):
                    pool.wait_ge(s_yst[par], 16 * ((TILES1 + 1 - par) // 2))
                pool.wait_ge(s_down, TILES1)
                for c in range(C):
                    if c >= RING:
                        pool.wait_ge(s_x1, c - RING + 1)
                    pool.indirect_dma_start(gbuf[:, c % RING, :], None, y1,
                                            bass.IndirectOffsetOnAxis(ap=slot1[:, c:c + 1], axis=0)
                                            ).then_inc(s_g1[c % RING], 16)
                    if c == RING + 3:
                        split_piece(1, 0, 1)
                for i in (1, 2):
                    split_piece(1, i, 1)
                pool.wait_ge(s_down, G_SH1)
                for i in range(3):
                    split_piece(0, i, SET_E)

                pool.wait_ge(s_slot2, 1)
                pool.wait_ge(s_zero2, 16 * FILLS)
                for c in range(C):
                    pool.wait_ge(s_row2[c % RING], 16 * (c // RING + 1))
                    for k in range(TOPK):
                        pool.indirect_dma_start(xs2, bass.IndirectOffsetOnAxis(ap=slot2[:, c, k:k + 1], axis=0),
                                                gbuf[:, c % RING, :], None).then_inc(s_scat2[c], 16)
                pool.wait_ge(s_down, G_RT)
                for i in range(3):
                    split_piece(1, i, SET_E + 1)

                def rest(n, buf, e):
                    pool.wait_ge(s_down, pool.value_load(tab_free[0:1, bass.ds(e, 1)], min_val=G_RT,
                                                         max_val=G_SH2))
                    for i in range(3):
                        split_piece(buf, i, n)
                with pool.Fori(0, (E2 - 2) // 2) as j:
                    rest(SET_E + 2 + 2 * j, 0, 2 * j)
                    rest(SET_E + 3 + 2 * j, 1, 2 * j + 1)
                rest(SET_SH2, 0, E2 - 2)

                for par in range(2):
                    pool.wait_ge(s_yst[par], 16 * stored_before((G_SH2 + (G_SH2 % 2 != par)) // 2, par))
                pool.wait_ge(s_down, G_SH2)
                for c in range(C):
                    if c >= 2:
                        pool.wait_ge(s_cmb, c - 1)
                    for k in range(TOPK):
                        pool.indirect_dma_start(gbuf[:, TOPK * (c % 2) + k, :], None, y2,
                                                bass.IndirectOffsetOnAxis(ap=slot2[:, c, k:k + 1], axis=0)
                                                ).then_inc(s_gy[c % 2], 16)
                    if c == 1:
                        split_piece(1, 0, SET_SH2 + 1)
                        split_piece(1, 1, SET_SH2 + 1)
                    elif c == 7:
                        split_piece(1, 2, SET_SH2 + 1)

            @block.scalar
            def _(a):
                def roots(n, tiles):
                    a.wait_ge(s_var, n + 1)
                    a.activation(std[:, 0:tiles], var[:, 0:tiles], ACT.Sqrt).then_inc(s_std, 1)
                for n in range(C // LN):
                    roots(n, LN)

                for e in range(E1):
                    for k in range(KD):
                        n = e * KD + k
                        a.wait_ge(s_ctp, n + 1)
                        a.activation(ct(e, 0)[:, k, :], ct_banks[n % 2][:], ACT.Copy).then_inc(s_cth, 1)
                a.wait_ge(s_wrp, 1)
                a.activation(wrT[:, 0], lg_ps[:, 0:KD * EL].rearrange("p (k e) -> p k e", k=KD),
                             ACT.Copy).then_inc(s_wrhi, 1)

                def load_rows(src, tile, par):
                    a.dma_start(xin[:, par, :].bitcast(F32), src[bass.ds(tile * P, P), :]).then_inc(s_in[par], 16)

                def hi_x(g, par):
                    a.wait_ge(s_xT, g + 1)
                    a.activation(hT[:, par, 0, :], xT_ps[:], ACT.Copy).then_inc(s_hhi, 1)

                def hi_a(g, chunks):
                    a.wait_ge(s_aT, g + 1)
                    if chunks[-1] == P:
                        n = len(chunks) * P
                        a.activation(aT[:, 0, 0:n], aT_ps[:, 0:n], ACT.Copy).then_inc(s_ahi, 1)
                    else:
                        m = chunks[-1]
                        a.activation(aT[:, 0, 0:2 * P], aT_ps[:, 0:2 * P], ACT.Copy)
                        a.activation(aT[0:m, 0, 2 * P:3 * P], aT_ps[0:m, 2 * P:3 * P], ACT.Copy).then_inc(s_ahi, 1)

                def do_silu(g, f):
                    a.wait_ge(s_gate, g + 1)
                    if not (isinstance(g, int) and g == 0):
                        a.wait_ge(s_act, g)
                    a.activation(silu[:, 0:f], g_ps[:, 0:f], ACT.Silu).then_inc(s_silu, 1)

                def y_copy(g, par, before):
                    a.wait_ge(s_down, g + 1)
                    if not (isinstance(before, int) and before == 0):
                        a.wait_ge(s_yst[par], 16 * before)
                    a.activation(ysb[:, par, :], y_ps[:], ACT.Copy).then_inc(s_y, 1)

                def y_store(dst, g, tile, par):
                    a.wait_ge(s_y, g + 1)
                    a.dma_start(dst[bass.ds(tile * P, P), :], ysb[:, par, :]).then_inc(s_yst[par], 16)

                for c in range(C):
                    a.wait_ge(s_scat1[c], 16)
                load_rows(xs1, 0, 0)
                load_rows(xs1, 1, 1)
                hi_x(0, 0)
                load_rows(xs1, 2, 0)
                hi_x(1, 1)
                load_rows(xs1, 3, 1)
                do_silu(0, F1)

                def layer1(loads, stores):
                    def body(g, half, par):
                        if stores:
                            y_store(y1, g - 2, g - 2, par)
                        hi_a(g - 1, CH1)
                        hi_x(g + 1, 1 - par)
                        if loads:
                            load_rows(xs1, g + 3, 1 - par)
                        do_silu(g, F1)
                        y_copy(g - 1, 1 - par, half - (1 - par))
                    return body
                last = TILES1 - 1
                layer1(True, False)(1, 0, 1)
                layer1(True, True)(2, 1, 0)
                run_steps(a, 3, last - 2, layer1(True, True))
                run_steps(a, last - 2, last, layer1(False, True))
                y_store(y1, last - 2, last - 2, last % 2)
                hi_a(last - 1, CH1)
                do_silu(last, F1)
                y_copy(last - 1, (last - 1) % 2, (last - 1) // 2)
                y_store(y1, last - 1, last - 1, (last - 1) % 2)
                hi_a(last, CH1)
                y_copy(last, last % 2, last // 2)
                y_store(y1, last, last, last % 2)

                first_ln = C // LN
                g = G_SH0
                roots(first_ln, 2)
                hi_x(g, g % 2)
                hi_x(g + 1, 1 - g % 2)
                roots(first_ln + 1, 2)
                do_silu(g, F2)

                def sum_start(c):
                    a.wait_ge(s_down, G_SH0 + c + 1)
                    a.wait_ge(s_h2st[c // 2], 32)
                    a.activation(h_all[:, c, :], y_ps[:], ACT.Copy).then_inc(s_y, 1)

                def load_h2(g, par):
                    load_rows(h2tok, g - G_SH1, par)
                for i in range(1, C + 1):
                    g = G_SH0 + i
                    hi_a(g - 1, CH2)
                    hi_x(g + 1, (g + 1) % 2)
                    if i % 2 == 0 and i <= C - 4:
                        roots(first_ln + i // 2 + 1, 2)
                    if i == C - 3:
                        for j in range(C // 2):
                            a.wait_ge(s_h2st[j], 32)
                    if i >= C - 3:
                        load_h2(g + 3, (g + 3) % 2)
                    do_silu(g, F2)
                    sum_start(i - 1)

                def layer2(first):
                    copies = G_RT <= first - 1 < G_SH2
                    stores = G_RT <= first - 2 < G_SH2
                    row = first + 3
                    src, base = next(((s, b) for s, b, e in (
                        (h2tok, G_SH1, G_RT), (xs2, G_RT, G_SH2), (h2tok, G_SH2, G_SH3),
                        (h2tok, G_SH2, G_SH3), (h2tok, G_SH3, G_END)) if b <= row < e), (None, 0))
                    if row in (G_RT, G_RT + 1):
                        src = None

                    def body(g, half, par):
                        if stores:
                            y_store(y2, g - 2, g - 2 - G_RT, par)
                        hi_a(g - 1, CH2)
                        hi_x(g + 1, 1 - par)
                        if src is not None:
                            load_rows(src, g + 3 - base, 1 - par)
                        do_silu(g, F2)
                        if copies:
                            y_copy(g - 1, 1 - par, stored_before(half - (1 - par), 1 - par))
                    return body

                cuts = [G_SH1 + 1, SHARES, G_RT - 3, G_RT - 1, G_RT + 1, G_RT + 2, G_SH2 - 3, G_SH2 + 1, G_SH2 + 2,
                        G_SH3 - 3, G_END - 3, G_END - 1]
                for first, end in zip(cuts, cuts[1:]):
                    if first == SHARES:
                        a.wait_ge(s_exin, 1)
                        a.activation(expo[:], expo[:], ACT.Exp).then_inc(s_exp, 1)
                        a.activation(etop[:], etop[:], ACT.Exp).then_inc(s_exp, 1)
                        a.activation(sgate[:], logits[:, :, E2], ACT.Sigmoid).then_inc(s_exp, 1)
                    if first == G_RT - 1:
                        for c in range(C):
                            a.wait_ge(s_scat2[c], 16 * TOPK)
                        load_rows(xs2, 0, G_RT % 2)
                        load_rows(xs2, 1, 1 - G_RT % 2)
                    run_steps(a, first, end, layer2(first))
                g = G_END - 1
                hi_a(g - 1, CH2)
                do_silu(g, F2)
                hi_a(g, CH2)

            @block.tensor
            def _(pe):
                pe.wait_ge(s_const, 9)
                def contexts(i):
                    pe.wait_ge(s_ctx[i], 32)
                    for e in (2 * i, 2 * i + 1):
                        for k in range(KD):
                            n = e * KD + k
                            if n >= 2:
                                pe.wait_ge(s_ctl, n - 1)
                            for f in range(KD):
                                last = pe.transpose(ct_banks[n % 2][:, f * P:(f + 1) * P],
                                                    raw_ctx(e)[:, f, k * P:(k + 1) * P], ident[:])
                            last.then_inc(s_ctp, 1)
                def ranks(width, s_mask, s_cum):
                    pe.wait_ge(s_mask, 1)
                    pe.matmul(cum_ps[:, 0:width], tri[:], maskb[:, 0:width], start=True, stop=True)
                    pe.matmul(tot_ps[:, 0:width], ones[:], maskb[:, 0:width], start=True,
                              stop=True).then_inc(s_cum, 1)
                ranks(C * E1, s_mask1, s_cum1)
                contexts(0)
                contexts(1)
                pe.wait_ge(s_wr, 32)
                for k in range(KD):
                    last = pe.transpose(lg_ps[:, k * EL:(k + 1) * EL], wr_rows[:, k * P:(k + 1) * P],
                                        ident[0:EL, 0:EL])
                last.then_inc(s_wrp, 1)

                def x_transposes(g, half, par, skipped=0):
                    pe.wait_ge(s_in[par], 16 * (half + 1 - skipped))
                    if not (isinstance(g, int) and g == 0):
                        pe.wait_ge(s_hT, g)
                    for k in range(KD):
                        last = pe.transpose(xT_ps[:, k * P:(k + 1) * P].bitcast(F32R), xin[:, par, k * P:(k + 1) * P],
                                            ident_r[:])
                    last.then_inc(s_xT, 1)

                def a_transposes(g, chunks):
                    pe.wait_ge(s_act, g + 1)
                    for k, m in enumerate(chunks):
                        last = pe.transpose(aT_ps[0:m, k * P:(k + 1) * P], act[:, k * P:k * P + m], ident[:])
                    last.then_inc(s_aT, 1)

                def product(ps, left, right, chunks, done):
                    n = 3 * len(chunks)
                    i = 0
                    for k, m in enumerate(chunks):
                        for l, r in ((0, 0), (0, 1), (1, 0)):
                            mm = pe.matmul(ps, left(l, k, m), right(r, k, m), start=(i == 0), stop=(i == n - 1))
                            i += 1
                    mm.then_inc(done, 1)

                def h_left(par):
                    return lambda l, k, m: hT[0:m, par, l, k * P:(k + 1) * P]

                def a_left(l, k, m):
                    return aT[0:m, l, k * P:(k + 1) * P]

                def context_of(g):
                    at = pe.value_load(tab1[0:1, bass.ds(g, 1)], min_val=0, max_val=2 * WSET + KD * F1)
                    return lambda r, k, m: wflat[:, bass.ds(at + (r * WSET + k * F1), F1)]

                def down1(g, right):
                    pe.wait_ge(s_aTs, g + 1)
                    if not (isinstance(g, int) and g == 0):
                        pe.wait_ge(s_y, g)
                    product(y_ps[:], a_left, right, CH1, s_down)

                def gate1(g, par, right):
                    pe.wait_ge(s_hT, g + 1)
                    product(g_ps[:], h_left(par), right, CH1, s_gate)

                pe.wait_ge(s_ctl, E1 * KD)
                pe.wait_ge(s_slot1, 1)
                x_transposes(0, 0, 0)
                x_transposes(1, 0, 1)
                gate1(0, 0, context_of(0))

                def layer1(g, half, par):
                    own, before = context_of(g), context_of(g - 1)
                    a_transposes(g - 1, CH1)
                    x_transposes(g + 1, half + (1 if par else 0), 1 - par)
                    gate1(g, par, own)
                    down1(g - 1, before)
                layer1(1, 0, 1)
                run_steps(pe, 2, TILES1 - 1, layer1)
                g = TILES1 - 1
                own, before = context_of(g), context_of(g - 1)
                a_transposes(g - 1, CH1)
                gate1(g, g % 2, own)
                down1(g - 1, before)
                a_transposes(g, CH1)
                down1(g, own)

                def set_right(at, part):
                    off, _, w = PIECES[part]
                    return lambda r, k, m: wflat[0:m, bass.ds(at + (r * WSET + off + k * w), w)]

                def gate_up(g, par, at, number):
                    pe.wait_ge(s_hT, g + 1)
                    pe.wait_ge(s_split[0], number)
                    product(g_ps[:, 0:F2], h_left(par), set_right(at, 0), [P] * KD, s_gate)
                    pe.wait_ge(s_split[1], number)
                    product(u_ps[:, 0:F2], h_left(par), set_right(at, 1), [P] * KD, s_up)
                    pe.wait_ge(s_split[2], number)

                def down2(g, at):
                    pe.wait_ge(s_aTs, g + 1)
                    pe.wait_ge(s_y, g)
                    product(y_ps[:], a_left, set_right(at, 2), CH2, s_down)

                def h_transposes(c):
                    pe.wait_ge(s_h2, c + 1)
                    pe.wait_ge(s_hT, G_SH0 + c)
                    for k in range(KD):
                        last = pe.transpose(xT_ps[:, k * P:(k + 1) * P], h_all[:, c, k * P:(k + 1) * P], ident[:])
                    last.then_inc(s_xT, 1)

                def router_product(c, par):
                    if c >= 2:
                        pe.wait_ge(s_lgs, c - 1)
                    product(lg_banks[c % 2][:, 0:EL], h_left(par), lambda r, k, m: wrT[:, r, k, :], [P] * KD,
                            s_lg)

                skipped = C // 2
                g = G_SH0
                h_transposes(0)
                h_transposes(1)
                gate_up(g, g % 2, 0, 1)
                pe.wait_ge(s_wrT, 1)
                router_product(0, g % 2)
                for c in range(1, C):
                    g = G_SH0 + c
                    a_transposes(g - 1, CH2)
                    if c < C - 1:
                        h_transposes(c + 1)
                    else:
                        x_transposes(g + 1, (g + 1) // 2, (g + 1) % 2, skipped)
                    gate_up(g, g % 2, 0, 1)
                    router_product(c, g % 2)
                    down2(g - 1, 0)

                def quarter1(g, half, par, before=2 * WSET):
                    a_transposes(g - 1, CH2)
                    x_transposes(g + 1, half + (1 if par else 0), 1 - par, skipped)
                    gate_up(g, par, 2 * WSET, 2)
                    if isinstance(g, int) and g == G_SH1:
                        ranks(C * E2, s_mask2, s_cum2)
                    down2(g - 1, before)
                g = G_SH1
                quarter1(g, g // 2, g % 2, before=0)
                run_steps(pe, G_SH1 + 1, G_RT, quarter1)
                pe.wait_ge(s_slot2, 1)

                def by_table(g, half, par, last=False):
                    row = g - G_RT
                    at = pe.value_load(tab_buf[0:1, bass.ds(row + 1, 1)], min_val=0, max_val=2 * WSET)
                    number = pe.value_load(tab_cnt[0:1, bass.ds(row, 1)], min_val=1, max_val=SET_SH2 + 2)
                    before = pe.value_load(tab_buf[0:1, bass.ds(row, 1)], min_val=0, max_val=2 * WSET)
                    a_transposes(g - 1, CH2)
                    if not last:
                        x_transposes(g + 1, half + (1 if par else 0), 1 - par, skipped)
                    gate_up(g, par, at, number)
                    down2(g - 1, before)
                run_steps(pe, G_RT, G_END - 1, by_table)
                g = G_END - 1
                by_table(g, g // 2, g % 2, last=True)
                a_transposes(g, CH2)
                down2(g, 2 * WSET)

            @block.vector
            def _(v):
                chained = [0]

                def step(ins):
                    chained[0] += 1
                    ins.then_inc(s_dve, 1)
                    v.wait_ge(s_dve, chained[0])

                def link(ins, k):
                    ins.then_inc(s_ln, 1)
                    v.wait_ge(s_ln, k)

                def variances(n, c0, tiles):
                    for i in range(tiles):
                        last = v.bn_stats(stats[:, i, :], x_all[:, c0 + i, :])
                    link(last, 7 * n + 1)
                    for i in range(tiles):
                        last = v.bn_aggr(mv[:, i, :], stats[:, i, :])
                    link(last, 7 * n + 2)
                    v.tensor_scalar(var[:, 0:tiles], mv[:, 0:tiles, 1], EPS, None, ALU.add).then_inc(s_var, 1)

                def normalise(n, c0, tiles, done):
                    r, t, w = rstd[:, 0:tiles], newton[:, 0:tiles], var[:, 0:tiles]
                    v.wait_ge(s_std, n + 1)
                    link(v.reciprocal(r, std[:, 0:tiles]), 7 * n + 3)
                    link(v.tensor_tensor(t, r, r, ALU.mult), 7 * n + 4)
                    link(v.tensor_tensor(t, t, w, ALU.mult), 7 * n + 5)
                    link(v.tensor_scalar(t, t, -0.5, 1.5, ALU.mult, ALU.add), 7 * n + 6)
                    link(v.tensor_tensor(r, r, t, ALU.mult), 7 * n + 7)
                    for i in range(tiles):
                        v.tensor_scalar(h_all[:, c0 + i, :], x_all[:, c0 + i, :], mv[:, i, 0:1],
                                        rstd[:, i:i + 1], ALU.subtract, ALU.mult).then_inc(done, 1)

                def slots(E, s_cum):
                    W = C * E
                    v.wait_ge(s_cum, 1)
                    tot_e = tot[:, 0:W].rearrange("p (e c) -> p e c", e=E)
                    run_e = run[:, 0:W].rearrange("p (e c) -> p e c", e=E)
                    step(v.tensor_copy(tot_e, tot_ps[:, 0:W].rearrange("p (c e) -> p e c", e=E)))
                    step(v.tensor_reduce(cnt[:, 0:E], tot_e, AX.X, ALU.add))
                    step(v.tensor_scalar(padi[:, 0:E], cnt[:, 0:E], float(P - 1), None, ALU.add))
                    step(v.tensor_scalar(padi[:, 0:E], padi[:, 0:E], 7, 7, ALU.arith_shift_right,
                                         ALU.arith_shift_left))
                    step(v.tensor_copy(padf[:, 0:E], padi[:, 0:E]))
                    step(v.tensor_tensor_scan(bend[:, 0:E], one_row[:, 0:E], padf[:, 0:E], 0.0, ALU.mult, ALU.add))
                    step(v.tensor_tensor_scan(cexc[:, 0:E], one_row[:, 0:E], cnt[:, 0:E], 0.0, ALU.mult, ALU.add))
                    step(v.tensor_tensor(cexc[:, 0:E], bend[:, 0:E], cexc[:, 0:E], ALU.subtract))
                    step(v.tensor_tensor(cexc[:, 0:E], cexc[:, 0:E], padf[:, 0:E], ALU.subtract))
                    step(v.tensor_tensor(cexc[:, 0:E], cexc[:, 0:E], cnt[:, 0:E], ALU.add))
                    step(v.tensor_tensor_scan(run[:, 0:W], one_row[:, 0:W], tot[:, 0:W], 0.0, ALU.mult, ALU.add))
                    step(v.tensor_tensor(run[:, 0:W], run[:, 0:W], tot[:, 0:W], ALU.subtract))
                    step(v.tensor_tensor(run_e, run_e, cexc[:, 0:E].unsqueeze(2).to_broadcast([P, E, C]), ALU.add))
                    step(v.tensor_tensor(vslot[:, :, 0:E], cum_ps[:, 0:W].rearrange("p (c e) -> p c e", e=E),
                                         run[:, 0:W].rearrange("p (e c) -> p c e", e=E), ALU.add))

                def experts_of_tiles(E, tiles):
                    step(v.tensor_scalar(bend[:, 0:E], bend[:, 0:E], 1.0 / P, None, ALU.mult))
                    step(v.tensor_tensor(cmp_t[:, 0:tiles, 0:E],
                                         bend[:, 0:E].unsqueeze(1).to_broadcast([P, tiles, E]),
                                         iota_t[:, 0:tiles].unsqueeze(2).to_broadcast([P, tiles, E]), ALU.is_le))
                    step(v.tensor_reduce(texp[:, 0:tiles], cmp_t[:, 0:tiles, 0:E], AX.X, ALU.add))
                    step(v.tensor_scalar(texp[:, 0:tiles], texp[:, 0:tiles], float(E - 1), None, ALU.min))

                one_row = expo[:].rearrange("p c e -> p (c e)")
                step(v.memset(one_row, 1.0))

                v.wait_ge(s_tok, 16)
                hot1 = hot[:, 0, :, 0:E1]
                ge = hot[:, 1, :, 0:E1 + 1]
                step(v.memset(ge[:, :, 0], 1.0))
                step(v.memset(ge[:, :, E1], 0.0))
                for e in range(1, E1):
                    step(v.tensor_scalar(ge[:, :, e], tokid[:], float(BOUND1 * e), None, ALU.is_ge))
                step(v.tensor_tensor(hot1, ge[:, :, 0:E1], ge[:, :, 1:E1 + 1], ALU.subtract))
                v.tensor_copy(maskb[:, 0:C * E1].rearrange("p (c e) -> p c e", e=E1), hot1).then_inc(s_mask1, 1)
                v.wait_ge(s_const, 9)
                slots(E1, s_cum1)
                experts_of_tiles(E1, TILES1)
                step(v.tensor_scalar(late[:], texp[0:1, 0:TILES1], 2.0, float(2 * WSET - 2 * KD * F1), ALU.is_ge,
                                     ALU.mult))
                step(v.scalar_tensor_tensor(out=tab1[:], in0=texp[0:1, 0:TILES1], scalar=float(KD * F1), in1=late[:],
                                            op0=ALU.mult, op1=ALU.add))
                step(v.tensor_scalar(tab_ct[:], bend[0:1, 1:2], 1.0, None, ALU.max))
                step(v.tensor_tensor(vslot[:, :, 0:E1], vslot[:, :, 0:E1], hot1, ALU.mult))
                step(v.tensor_reduce(slotf[:, :, 0], vslot[:, :, 0:E1], AX.X, ALU.add))
                v.tensor_copy(slot1[:], slotf[:, :, 0]).then_inc(s_slot1, 1)

                for i in range(C // LN):
                    v.wait_ge(s_x[i], 16)
                    variances(i, LN * i, LN)
                    normalise(i, LN * i, LN, s_h1)

                for e in range(E1):
                    for k in range(KD):
                        n = e * KD + k
                        v.wait_ge(s_cth, n + 1)
                        v.tensor_tensor(ct(e, 1)[:, k, :], ct_banks[n % 2][:], ct(e, 0)[:, k, :].bitcast(F32),
                                        ALU.subtract).then_inc(s_ctl, 1)

                v.wait_ge(s_wrhi, 1)
                v.tensor_tensor(wrT[:, 1], lg_ps[:, 0:KD * EL].rearrange("p (k e) -> p k e", k=KD),
                                wrT[:, 0].bitcast(F32), ALU.subtract).then_inc(s_wrT, 1)

                def lo_x(g, par):
                    v.wait_ge(s_hhi, g + 1)
                    v.tensor_tensor(hT[:, par, 1, :], xT_ps[:], hT[:, par, 0, :].bitcast(F32),
                                    ALU.subtract).then_inc(s_hT, 1)

                def lo_a(g, chunks):
                    v.wait_ge(s_ahi, g + 1)
                    if chunks[-1] == P:
                        n = len(chunks) * P
                        v.tensor_tensor(aT[:, 1, 0:n], aT_ps[:, 0:n], aT[:, 0, 0:n].bitcast(F32),
                                        ALU.subtract).then_inc(s_aTs, 1)
                    else:
                        m = chunks[-1]
                        v.tensor_tensor(aT[:, 1, 0:2 * P], aT_ps[:, 0:2 * P], aT[:, 0, 0:2 * P].bitcast(F32),
                                        ALU.subtract)
                        v.tensor_tensor(aT[0:m, 1, 2 * P:3 * P], aT_ps[0:m, 2 * P:3 * P],
                                        aT[0:m, 0, 2 * P:3 * P].bitcast(F32), ALU.subtract).then_inc(s_aTs, 1)

                def act1(g):
                    v.wait_ge(s_silu, g + 1)
                    v.tensor_tensor(act[:], g_ps[:], silu[:], ALU.mult).then_inc(s_act, 1)

                def act2(g):
                    v.wait_ge(s_silu, g + 1)
                    v.wait_ge(s_up, g + 1 - TILES1)
                    v.tensor_tensor(act[:, 0:F2], u_ps[:, 0:F2], silu[:, 0:F2], ALU.mult).then_inc(s_act, 1)

                lo_x(0, 0)
                lo_x(1, 1)
                act1(0)

                def layer1(g, half, par):
                    lo_a(g - 1, CH1)
                    lo_x(g + 1, 1 - par)
                    act1(g)
                run_steps(v, 1, TILES1 - 1, layer1)
                g = TILES1 - 1
                lo_a(g - 1, CH1)
                act1(g)
                lo_a(g, CH1)

                first_ln = C // LN
                def residual(j):
                    for c in (2 * j, 2 * j + 1):
                        v.wait_ge(s_g1[c % RING], 16 * (c // RING + 1))
                        v.tensor_tensor(x_all[:, c, :], x_all[:, c, :], gbuf[:, c % RING, :],
                                        ALU.add).then_inc(s_x1, 1)
                    v.wait_ge(s_x1, 2 * j + 2)
                    variances(first_ln + j, 2 * j, 2)

                def rows(j):
                    normalise(first_ln + j, 2 * j, 2, s_h2)

                def top(c):
                    v.wait_ge(s_lg, c + 1)
                    v.tensor_copy(logits[:, c, :], lg_banks[c % 2][:, 0:EL]).then_inc(s_lgs, 1)
                    v.wait_ge(s_lgs, c + 1)
                    step(v.max(top8[:, c, :], logits[:, c, 0:E2]))
                    v.max_index(idx8[:, c, :], top8[:, c, :], logits[:, c, 0:E2]).then_inc(s_top, 1)

                g = G_SH0
                residual(0)
                rows(0)
                residual(1)
                lo_x(g, g % 2)
                lo_x(g + 1, 1 - g % 2)
                rows(1)
                act2(g)
                for i in range(1, C):
                    g = G_SH0 + i
                    lo_a(g - 1, CH2)
                    lo_x(g + 1, 1 - g % 2)
                    if i % 2 == 0 and i <= C - 4:
                        rows(i // 2 + 1)
                    act2(g)
                    if i % 2 and i <= C - 5:
                        residual((i + 3) // 2)
                    top(i - 1)

                def add_y(g, c):
                    v.wait_ge(s_down, g + 1)
                    v.tensor_tensor(tile_of(h_all, c), y_ps[:], tile_of(h_all, c), ALU.add).then_inc(s_y, 1)

                def masks():
                    v.wait_ge(s_top, C)
                    step(v.tensor_copy(idxf[:], idx8[:, :, 0:TOPK]))
                    for k in range(TOPK):
                        last = v.tensor_tensor(hot[:, k], iota_e[:].unsqueeze(1).to_broadcast([P, C, E2]),
                                               idxf[:, :, k:k + 1].to_broadcast([P, C, E2]), ALU.is_equal)
                    step(last)
                    step(v.tensor_tensor(vslot[:], hot[:, 0], hot[:, 1], ALU.add))
                    step(v.tensor_tensor(vslot[:], vslot[:], hot[:, 2], ALU.add))
                    v.tensor_tensor(maskb[:].rearrange("p (c e) -> p c e", e=E2), vslot[:], hot[:, 3],
                                    ALU.add).then_inc(s_mask2, 1)

                def slots_of(ks):
                    one_hot_sum = run[:].rearrange("p (c e) -> p c e", e=E2)
                    for k in ks:
                        step(v.tensor_tensor(one_hot_sum, hot[:, k], vslot[:], ALU.mult))
                        step(v.tensor_reduce(slotf[:, :, k], one_hot_sum, AX.X, ALU.add))

                def tables():
                    step(v.tensor_copy(slot2[:], slotf[:]))
                    sets = slice(1, 1 + TILES2)
                    step(v.memset(tab_buf[:, 0:1], 2 * WSET))
                    step(v.tensor_scalar(tab_cnt[:, 0:TILES2], texp[0:1, :], float(SET_E + 1), None, ALU.add))
                    step(v.tensor_copy(texi[0:1, :], texp[0:1, :]))
                    step(v.tensor_scalar(texi[0:1, :], texi[0:1, :], 1, None, ALU.bitwise_and))
                    step(v.tensor_scalar(tab_buf[:, sets], texi[0:1, :], float(2 * WSET), None, ALU.mult))
                    for i in range(2):
                        step(v.memset(tab_buf[:, 1 + TILES2 + i * C:1 + TILES2 + (i + 1) * C], i * 2 * WSET))
                        step(v.memset(tab_cnt[:, TILES2 + i * C:TILES2 + (i + 1) * C], SET_SH2 + i + 1))
                    v.tensor_scalar(tab_free[:], bend[0:1, :], float(G_RT), None, ALU.add).then_inc(s_slot2, 1)

                def exponents():
                    step(v.tensor_tensor(etop[:], top8[:, :, 0:TOPK], top8[:, :, 0:1].to_broadcast([P, C, TOPK]),
                                         ALU.subtract))
                    v.tensor_tensor(expo[:], logits[:, :, 0:E2], top8[:, :, 0:1].to_broadcast([P, C, E2]),
                                    ALU.subtract).then_inc(s_exin, 1)

                def shares():
                    v.wait_ge(s_exp, 3)
                    step(v.tensor_reduce(zsum[:], expo[:], AX.X, ALU.add))
                    step(v.reciprocal(zsum[:], zsum[:]))
                    step(v.tensor_tensor(etop[:], etop[:], zsum[:].unsqueeze(2).to_broadcast([P, C, TOPK]), ALU.mult))
                    step(v.tensor_reduce(zsum[:], etop[:], AX.X, ALU.add))
                    step(v.tensor_scalar(zsum[:], zsum[:], 1e-9, None, ALU.max))
                    step(v.reciprocal(zsum[:], zsum[:]))
                    step(v.tensor_tensor(combw[:], etop[:], zsum[:].unsqueeze(2).to_broadcast([P, C, TOPK]), ALU.mult))

                def halves(g, par):
                    lo_a(g - 1, CH2)
                    lo_x(g + 1, 1 - par)
                    act2(g)

                g = G_SH1
                lo_a(g - 1, CH2)
                lo_x(g + 1, 1 - g % 2)
                top(C - 1)
                masks()
                act2(g)
                slots(E2, s_cum2)
                for i in range(1, SHARES - G_SH1 + 1):
                    g = G_SH1 + i
                    lo_a(g - 1, CH2)
                    lo_x(g + 1, 1 - g % 2)
                    if i == 1:
                        slots_of((0, 1))
                    elif i == 2:
                        experts_of_tiles(E2, TILES2)
                    act2(g)
                    add_y(g - 1, i - 1)
                    if i == 1:
                        slots_of((2, 3))
                    elif i == 2:
                        tables()
                    elif i == 3:
                        exponents()
                    elif g == SHARES:
                        shares()

                def with_sum(c0):
                    def body(g, half, par):
                        halves(g, par)
                        add_y(g - 1, g - c0)
                    return body
                run_steps(v, SHARES + 1, G_RT + 1, with_sum(G_SH1 + 1))

                run_steps(v, G_RT + 1, G_SH2 + 1, lambda g, half, par: halves(g, par))

                def combine(c, par, turn, ks):
                    if ks[0] == 0:
                        v.wait_ge(s_gy[par], 16 * TOPK * (turn + 1))
                    row = tile_of(x_all, c)
                    for k in ks:
                        if k:
                            v.wait_ge(s_cstep, 3 * c + k)
                        ins = v.scalar_tensor_tensor(
                            out=row, in0=gbuf[:, TOPK * par + k, :],
                            scalar=combw[:, bass.ds(c, 1), k:k + 1].rearrange("p a k -> p (a k)"),
                            in1=row, op0=ALU.mult, op1=ALU.add)
                        ins.then_inc(s_cmb if k == TOPK - 1 else s_cstep, 1)

                run_steps(v, G_SH2 + 1, COMBINE, with_sum(G_SH2 + 1))
                ahead = COMBINE - G_SH2 - 1

                def combining(c, par, turn):
                    g, gpar = COMBINE + c, (COMBINE + par) % 2
                    lo_a(g - 1, CH2)
                    lo_x(g + 1, 1 - gpar)
                    combine(c, par, turn, (0, 1, 2))
                    act2(g)
                    combine(c, par, turn, (3,))
                with v.Fori(0, (C - ahead) // 2) as j:
                    for u in range(2):
                        combining(2 * j + u, u, j)
                        add_y(COMBINE + u - 1 + 2 * j, ahead + u + 2 * j)

                def last_sum(g, c):
                    v.wait_ge(s_down, g + 1)
                    v.tensor_tensor(tile_of(h_all, c), y_ps[:], tile_of(h_all, c), ALU.add).then_inc(s_y, 1)
                    v.wait_ge(s_y, g + 1)
                    gate = sgate[:, c:c + 1] if isinstance(c, int) else sgate[:, bass.ds(c, 1)]
                    row = tile_of(x_all, c)
                    v.scalar_tensor_tensor(out=row, in0=tile_of(h_all, c), scalar=gate, in1=row, op0=ALU.mult,
                                           op1=ALU.add).then_inc(s_fin, 1)

                for c in range(C - ahead, C):
                    combining(c, c % 2, c // 2)
                    last_sum(COMBINE + c - 1, c - C + ahead)

                def final(g, half, par):
                    halves(g, par)
                    last_sum(g - 1, g - 1 - G_SH3)
                run_steps(v, G_SH3 + 1 + ahead, G_END - 1, final)
                g = G_END - 1
                lo_a(g - 1, CH2)
                act2(g)
                last_sum(g - 1, C - 2)
                lo_a(g, CH2)
                last_sum(g, C - 1)


_INS = ["x", "itok_BxS_13_99985", "ctx_2048", "L0_ffn_router_w", "L0_ffn_w_gate", "L0_ffn_w_up", "L0_ffn_w_down",
        "L0_ffn_sh_gate", "L0_ffn_sh_up", "L0_ffn_sh_down", "L0_ffn_sh_gate_w"]

_OUTS = [((4, 512, 512), "float32")]


def kernel(**inputs):
    import numpy as _np
    import concourse.bacc as _bacc
    from concourse import mybir as _mybir
    from concourse.bass_utils import run_bass_kernel_spmd as _run

    nc = _bacc.Bacc("TRN2", target_bir_lowering=False, num_devices=1)
    arrays, args = {}, []
    for name in _INS:
        a = _np.ascontiguousarray(inputs[name])
        arrays[f"in_{name}_dram"] = a
        args.append(nc.dram_tensor(f"in_{name}_dram", a.shape, _mybir.dt.from_np(a.dtype), kind="ExternalInput").ap())
    for i, (shape, dtype) in enumerate(_OUTS):
        dt = _mybir.dt.from_np(_np.dtype(dtype))
        args.append(nc.dram_tensor(f"out_{i}_dram", shape, dt, kind="ExternalOutput").ap())
    build(nc, *args)
    r = _run(nc, [arrays], core_ids=[0])
    return r.results[0]["out_0_dram"]
```

```python
from contextlib import ExitStack

import concourse.bass as bass
from concourse import mybir

F32 = mybir.dt.float32
F32R = mybir.dt.float32r
BF16 = mybir.dt.bfloat16
I32 = mybir.dt.int32
U32 = mybir.dt.uint32
ALU = mybir.AluOpType
ACT = mybir.ActivationFunctionType
AX = mybir.AxisListType

P = 128
D = 512
KD = D // P
NTOK = 2048
C = NTOK // P
E1, F1 = 4, 512
BOUND1 = 6250
TILES1 = NTOK // P + E1 - 1
E2, F2, TOPK = 16, 352, 4
QUARTERS = 4
TILES2 = NTOK * TOPK // P + E2 - 1
CH1 = [P] * (F1 // P)
CH2 = [P, P, F2 - 2 * P]
WG, WU, WD = 0, KD * F2, 2 * KD * F2
WSET = 2 * KD * F2 + len(CH2) * D
EPS = 1e-5
LN = 4

G_SH0 = TILES1
G_SH1 = G_SH0 + C
G_RT = G_SH1 + C
G_SH2 = G_RT + TILES2
G_SH3 = G_SH2 + C
G_END = G_SH3 + C
SET_E = 2
SET_SH2 = SET_E + E2
EL = 18
RING = 8
FREE1 = TILES1 - C
FREE2 = TILES2 - C * TOPK
ZEROS2 = (4, 7, 11, FREE2)
SHARES = G_SH1 + 8
COMBINE = G_SH2 + 3


def run_steps(eng, first, end, body):
    pairs = (end - first) // 2
    if pairs > 1:
        with eng.Fori(0, pairs) as j:
            for u in range(2):
                body(first + u + 2 * j, (first + u) // 2 + j, (first + u) % 2)
    elif pairs == 1:
        for u in range(2):
            body(first + u, (first + u) // 2, (first + u) % 2)
    if (end - first) % 2:
        body(end - 1, (end - 1) // 2, (end - 1) % 2)


def build(nc, x, tok, ctx1, router_w, w_gate, w_up, w_down, sh_gate, sh_up, sh_down, sh_gate_w, out):
    x_v = x.rearrange("b s d -> (b s) d").rearrange("(p c) d -> p c d", c=C)
    out_v = out.rearrange("b s d -> (b s) d").rearrange("(p c) d -> p c d", c=C)
    tok_v = tok.rearrange("b s -> (b s)").rearrange("(p c) -> p c", c=C)

    with ExitStack() as ctx:
        def sb(name, shape, dt=F32):
            return ctx.enter_context(nc.sbuf_tensor(name, shape, dt))

        def dram(name, tiles):
            return nc.dram_tensor(name, [tiles * P, D], F32, kind="Internal").ap()

        def sem(name):
            return ctx.enter_context(nc.semaphore(name))

        xs1 = dram("xs1", TILES1)
        y1 = dram("y1", TILES1)
        h2tok = dram("h2tok", C)
        xs2 = dram("xs2", TILES2)
        y2 = dram("y2", TILES2)

        wset = sb("wset", [P, 2, 2, WSET], F32R)
        raw = sb("raw", [P, WSET])
        x_all = sb("x_all", [P, C, D])
        h_all = sb("h_all", [P, C, D])
        xin = sb("xin", [P, 2, D], F32R)
        hT = sb("hT", [P, 2, 2, KD * P], F32R)
        silu = sb("silu", [P, F1])
        act = sb("act", [P, F1])
        aT = sb("aT", [P, 2, len(CH1) * P], F32R)
        ysb = sb("ysb", [P, 2, D])
        gbuf = sb("gbuf", [P, RING, D])
        zeros = sb("zeros", [P, D])
        ident = sb("ident", [P, P])
        ident_r = sb("ident_r", [P, P], F32R)
        tri = sb("tri", [P, P], BF16)
        ones = sb("ones", [P, P], BF16)
        tokid = sb("tokid", [P, C], I32)
        wr_rows = sb("wr_rows", [EL, D])
        wrT = sb("wrT", [P, KD, 2, EL], F32R)
        stats = sb("stats", [P, LN, 6])
        mv = sb("mv", [P, LN, 2])
        var = sb("var", [P, LN])
        std = sb("std", [P, LN])
        rstd = sb("rstd", [P, 2, LN])
        newton = sb("newton", [P, LN])
        shift = sb("shift", [P, 2, LN])
        logits = sb("logits", [P, C, EL])
        top8 = sb("top8", [P, C, 8])
        idx8 = sb("idx8", [P, C, 8], U32)
        idxf = sb("idxf", [P, C, TOPK])
        expo = sb("expo", [P, C, E2])
        etop = sb("etop", [P, C, TOPK])
        combw = sb("combw", [P, C, TOPK])
        zsum = sb("zsum", [P, C])
        sgate = sb("sgate", [P, C])
        hot = gbuf[:, RING - 2:RING, :].rearrange("p a (b c e) -> p (a b) c e", c=C, e=E2)
        maskb = sb("maskb", [P, C * E2], BF16)
        tot = sb("tot", [P, E2 * C])
        run = sb("run", [P, E2 * C])
        vslot = sb("vslot", [P, C, E2])
        cnt = sb("cnt", [P, E2])
        cexc = sb("cexc", [P, E2])
        padi = sb("padi", [P, E2], I32)
        padf = sb("padf", [P, E2])
        bend = sb("bend", [P, E2])
        slotf = sb("slotf", [P, C, TOPK])
        slot1 = sb("slot1", [P, C], U32)
        freef = sb("freef", [P, FREE2])
        free1 = sb("free1", [P, FREE1], U32)
        free2 = sb("free2", [P, FREE2], U32)
        iota_free = sb("iota_free", [P, FREE2])
        slot2 = sb("slot2", [P, C, TOPK], U32)
        iota_e = sb("iota_e", [P, E2])
        iota_t = sb("iota_t", [P, TILES2])
        texp = sb("texp", [P, TILES2])
        late = sb("late", [1, TILES1])
        texi = sb("texi", [P, TILES2], I32)
        tab1 = sb("tab1", [1, TILES1], I32)
        tab_buf = sb("tab_buf", [1, 1 + TILES2], I32)
        tab_cnt = sb("tab_cnt", [1, TILES2], I32)
        tab_free = sb("tab_free", [1, E2], I32)
        tab_ct = sb("tab_ct", [1, 1], I32)
        cmp_t = ysb[:].rearrange("p a d -> p (a d)").rearrange("p (t e) -> p t e", e=E2)

        def bank(name):
            return ctx.enter_context(nc.psum_tensor(name, [P, 512], F32))
        xT_ps, g_ps, u_ps, aT_ps, y_ps, lg_ps, cum_ps, tot_ps = [
            bank(n) for n in ("xT_ps", "g_ps", "u_ps", "aT_ps", "y_ps", "lg_ps", "cum_ps", "tot_ps")]
        ct_banks = [g_ps, u_ps, aT_ps, y_ps]
        lg_banks = [lg_ps, cum_ps]

        s_const = sem("s_const")
        s_tok = sem("s_tok")
        s_x = [sem(f"s_xq{i}") for i in range(4)]
        s_wr = sem("s_wr")
        s_ctx = [sem(f"s_ctx{e}") for e in range(E1)]
        s_zero1 = sem("s_zero1")
        s_zero2 = [sem(f"s_zero2_{i}") for i in range(len(ZEROS2))]
        s_ln = sem("s_ln")
        s_var = sem("s_var")
        s_std = sem("s_std")
        s_affine = sem("s_affine")
        s_h1 = sem("s_h1")
        s_dve = sem("s_dve")
        s_mask1 = sem("s_mask1")
        s_mask2 = sem("s_mask2")
        s_cum1 = sem("s_cum1")
        s_cum2 = sem("s_cum2")
        s_free1 = sem("s_free1")
        s_free2 = sem("s_free2")
        s_slot1 = sem("s_slot1")
        s_slot2 = sem("s_slot2")
        s_tab2 = sem("s_tab2")
        s_scat1 = [sem(f"s_scat1_{c}") for c in range(C)]
        s_scat2 = [sem(f"s_scat2_{c}") for c in range(C)]
        s_ctp = sem("s_ctp")
        s_cth = sem("s_cth")
        s_ctl = sem("s_ctl")
        s_wrz = sem("s_wrz")
        s_wrp = sem("s_wrp")
        s_wrhi = sem("s_wrhi")
        s_wrT = sem("s_wrT")
        s_in = [sem(f"s_in{i}") for i in range(2)]
        s_xT = sem("s_xT")
        s_hhi = sem("s_hhi")
        s_hT = sem("s_hT")
        s_gate = sem("s_gate")
        s_up = sem("s_up")
        s_silu = sem("s_silu")
        s_act = sem("s_act")
        s_aT = sem("s_aT")
        s_ahi = sem("s_ahi")
        s_aTs = sem("s_aTs")
        s_down = sem("s_down")
        s_y = sem("s_y")
        s_yst = [sem(f"s_yst{i}") for i in range(2)]
        s_g1 = [sem(f"s_g1_{i}") for i in range(RING)]
        s_x1 = sem("s_x1")
        s_h2 = sem("s_h2")
        s_h2st = [sem(f"s_h2st{j}") for j in range(C // 2)]
        s_row2 = [sem(f"s_row2_{i}") for i in range(RING)]
        s_lg = sem("s_lg")
        s_lgs = sem("s_lgs")
        s_top = sem("s_top")
        s_exin = sem("s_exin")
        s_exp = sem("s_exp")
        s_raw = [sem(f"s_raw{i}") for i in range(3)]
        s_split = [sem(f"s_split{i}") for i in range(3)]
        s_pool = sem("s_pool")
        s_gy = [sem(f"s_gy{i}") for i in range(2)]
        s_cmb = sem("s_cmb")
        s_cstep = sem("s_cstep")
        s_out = sem("s_out")
        s_fin = sem("s_fin")

        PIECES = [(WG, KD, F2), (WU, KD, F2), (WD, len(CH2), D)]

        wflat = wset[:].rearrange("p b h w -> p (b h w)")

        def ct(e, part):
            return wset[:, e // 2, part, (e % 2) * KD * F1:(e % 2 + 1) * KD * F1].rearrange(
                "p (k f) -> p k f", k=KD)

        def raw_ctx(e):
            o = (e % 2) * KD * F1
            return raw[:, o:o + KD * F1].rearrange("p (k f) -> p k f", k=KD)

        def tile_of(rows, c):
            if isinstance(c, int):
                return rows[:, c, :]
            return rows[:, bass.ds(c, 1), :].rearrange("p a d -> p (a d)")

        def stored_before(half, par):
            in_layer1 = (TILES1 + 1 - par) // 2
            first = G_RT + (G_RT % 2 != par)
            return in_layer1 + half - first // 2

        with nc.Block() as block:

            @block.sync
            def _(sp):
                def load_set(n, gate, up, down):
                    for i, src in enumerate((gate, up)):
                        off, k, w = PIECES[i]
                        if not (isinstance(n, int) and n == 0):
                            sp.wait_ge(s_split[i], n)
                        sp.dma_start(raw[:, off:off + k * w].rearrange("p (k f) -> p k f", k=k),
                                     src).then_inc(s_raw[i], 16)
                    off = PIECES[2][0]
                    if not (isinstance(n, int) and n == 0):
                        sp.wait_ge(s_split[2], n)
                    sp.dma_start(raw[:, off:off + 2 * D].rearrange("p (k f) -> p k f", k=2),
                                 down[0:2 * P, :].rearrange("(k p) f -> p k f", p=P)).then_inc(s_raw[2], 16)
                    sp.dma_start(raw[0:CH2[2], off + 2 * D:off + 3 * D],
                                 down[2 * P:F2, :]).then_inc(s_raw[2], 16)

                def load_quarter(i, n):
                    cols = slice(i * F2, (i + 1) * F2)
                    load_set(n, sh_gate[:, cols].rearrange("(k p) f -> p k f", p=P),
                             sh_up[:, cols].rearrange("(k p) f -> p k f", p=P), sh_down[cols, :])

                def load_expert(e, n):
                    one = slice(e, e + 1) if isinstance(e, int) else bass.ds(e, 1)
                    load_set(n, w_gate[one].rearrange("e (k p) f -> p (e k) f", p=P),
                             w_up[one].rearrange("e (k p) f -> p (e k) f", p=P),
                             w_down[one].rearrange("e r f -> (e r) f"))

                def load_x(i):
                    sp.dma_start(x_all[:, 4 * i:4 * i + 4, :], x_v[:, 4 * i:4 * i + 4, :]).then_inc(s_x[i], 16)

                def load_ctx(e):
                    sp.dma_start(raw_ctx(e), ctx1[e].rearrange("(k p) f -> p k f", p=P)).then_inc(s_ctx[e], 16)
                sp.dma_start(tokid[:], tok_v).then_inc(s_tok, 16)
                load_x(0)
                load_ctx(0)
                load_x(1)
                load_ctx(1)
                load_x(2)
                load_x(3)
                sp.wait_ge(s_wrz, 1)
                sp.dma_start(wr_rows[0:E2, :], router_w).then_inc(s_wr, 16)
                sp.dma_start(wr_rows[E2:E2 + 1, :], sh_gate_w.rearrange("d o -> o d")).then_inc(s_wr, 16)
                for e in (2, 3):
                    sp.wait_ge(s_ctp, KD * (e - 1))
                    load_ctx(e)

                def first_rows(src, g):
                    for i in range(2):
                        sp.dma_start(xin[:, (g + i) % 2, :].bitcast(F32),
                                     src[i * P:(i + 1) * P, :]).then_inc(s_in[(g + i) % 2], 16)
                for c in range(C):
                    sp.wait_ge(s_scat1[c], 16)
                sp.wait_ge(s_zero1, 16 * FREE1)
                first_rows(xs1, 0)
                for par in range(2):
                    sp.wait_ge(s_in[par], 16)
                sp.wait_ge(s_ctp, E1 * KD)
                load_quarter(0, 0)
                load_quarter(1, 1)
                for c in range(C):
                    sp.wait_ge(s_h2, c + 1)
                    sp.dma_start(h2tok[c * P:(c + 1) * P, :], h_all[:, c, :]).then_inc(s_h2st[c // 2], 16)
                    if c == C - 5:
                        load_expert(0, SET_E)
                def row_back(c):
                    sp.dma_start(gbuf[:, c % RING, :], h2tok[c * P:(c + 1) * P, :]).then_inc(s_row2[c % RING], 16)
                for j in range(C // 2):
                    sp.wait_ge(s_h2st[j], 32)
                sp.wait_ge(s_x1, C)
                for c in range(RING - 2):
                    row_back(c)
                sp.wait_ge(s_slot2, 1)
                for c in range(RING - 2, RING):
                    row_back(c)
                for c in range(RING, C):
                    sp.wait_ge(s_scat2[c - RING], 16 * TOPK)
                    row_back(c)
                for c in range(C):
                    sp.wait_ge(s_scat2[c], 16 * TOPK)
                sp.wait_ge(s_zero2[0], 16 * ZEROS2[0])
                sp.wait_ge(s_xT, G_RT)
                first_rows(xs2, G_RT)
                load_expert(1, SET_E + 1)
                with sp.Fori(0, E2 - 2) as j:
                    load_expert(j + 2, j + SET_E + 2)
                for i in range(2, QUARTERS):
                    load_quarter(i, SET_SH2 + i - 2)
                for c in range(C):
                    sp.wait_ge(s_fin, c + 1)
                    sp.dma_start(out_v[:, c, :], x_all[:, c, :]).then_inc(s_out, 16)
                sp.wait_ge(s_out, 16 * C)

            @block.gpsimd
            def _(pool):
                pool.memset(zeros[:], 0.0).then_inc(s_const, 1)
                pool.memset(wr_rows[:], 0.0).then_inc(s_wrz, 1)
                pool.memset(ident[:], 0.0).then_inc(s_const, 1)
                pool.memset(tri[:], 1.0).then_inc(s_const, 1)
                pool.memset(ones[:], 1.0).then_inc(s_const, 1)
                pool.iota(iota_e[:], [[1, E2]], base=0, channel_multiplier=0,
                          allow_small_or_imprecise_dtypes=True).then_inc(s_const, 1)
                pool.iota(iota_t[:], [[1, TILES2]], base=0, channel_multiplier=0,
                          allow_small_or_imprecise_dtypes=True).then_inc(s_const, 1)
                pool.iota(iota_free[:], [[P, FREE2]], base=0, channel_multiplier=1,
                          allow_small_or_imprecise_dtypes=True).then_inc(s_const, 1)
                pool.wait_ge(s_const, 7)
                pool.affine_select(out=ident_r[:], in_=ident[:], compare_op=ALU.not_equal, fill=1.0, base=0,
                                   pattern=[[-1, P]], channel_multiplier=1).then_inc(s_const, 1)
                pool.wait_ge(s_const, 8)
                pool.affine_select(out=ident[:], in_=ident[:], compare_op=ALU.not_equal, fill=1.0, base=0,
                                   pattern=[[-1, P]], channel_multiplier=1).then_inc(s_const, 1)
                pool.affine_select(out=tri[:], in_=tri[:], compare_op=ALU.is_gt, fill=0.0, base=0,
                                   pattern=[[1, P]], channel_multiplier=-1).then_inc(s_const, 1)

                pool.wait_ge(s_free1, 1)
                for i in range(FREE1):
                    pool.indirect_dma_start(xs1, bass.IndirectOffsetOnAxis(ap=free1[:, i:i + 1], axis=0),
                                            zeros[:], None).then_inc(s_zero1, 16)
                pool.wait_ge(s_slot1, 1)
                for c in range(C):
                    pool.wait_ge(s_h1, c + 1)
                    pool.indirect_dma_start(xs1, bass.IndirectOffsetOnAxis(ap=slot1[:, c:c + 1], axis=0),
                                            h_all[:, c, :], None).then_inc(s_scat1[c], 16)

                def piece(buf, i):
                    off, k, w = PIECES[i]
                    return (wset[:, buf, 0, off:off + k * w], wset[:, buf, 1, off:off + k * w],
                            raw[:, off:off + k * w])

                def views(buf, i):
                    hi, lo, r = piece(buf, i)
                    if i < 2:
                        return [(hi, lo, r)]
                    m = CH2[2]
                    return [(hi[:, 0:2 * D], lo[:, 0:2 * D], r[:, 0:2 * D]),
                            (hi[0:m, 2 * D:], lo[0:m, 2 * D:], r[0:m, 2 * D:])]

                def split_piece(buf, i, n):
                    pool.wait_ge(s_raw[i], 16 * (n + 1) * (1 + (i == 2)))
                    parts = views(buf, i)
                    for hi, lo, r in parts:
                        zero = zeros[0:r.shape[0], 0:1].to_broadcast(list(r.shape))
                        last = pool.tensor_tensor(hi, r, zero, ALU.add)
                    last.then_inc(s_pool, 1)
                    pool.wait_ge(s_pool, 3 * n + i + 1)
                    for hi, lo, r in parts:
                        last = pool.tensor_tensor(lo, r, hi.bitcast(F32), ALU.subtract)
                    last.then_inc(s_split[i], 1)

                pool.wait_ge(s_down, pool.value_load(tab_ct[0:1, 0:1], min_val=1, max_val=TILES1))
                for i in range(3):
                    split_piece(0, i, 0)

                for par in range(2):
                    pool.wait_ge(s_yst[par], 16 * ((TILES1 + 1 - par) // 2))
                pool.wait_ge(s_down, TILES1)
                for c in range(C):
                    if c >= RING:
                        pool.wait_ge(s_x1, c - RING + 1)
                    pool.indirect_dma_start(gbuf[:, c % RING, :], None, y1,
                                            bass.IndirectOffsetOnAxis(ap=slot1[:, c:c + 1], axis=0)
                                            ).then_inc(s_g1[c % RING], 16)
                    if c == RING + 3:
                        split_piece(1, 0, 1)
                for i in (1, 2):
                    split_piece(1, i, 1)
                pool.wait_ge(s_down, G_SH1)
                for i in range(2):
                    split_piece(0, i, SET_E)

                def zeros_to_xs2(i):
                    for j in range(ZEROS2[i - 1] if i else 0, ZEROS2[i]):
                        pool.indirect_dma_start(xs2, bass.IndirectOffsetOnAxis(ap=free2[:, j:j + 1], axis=0),
                                                zeros[:], None).then_inc(s_zero2[i], 16)
                pool.wait_ge(s_free2, 1)
                zeros_to_xs2(0)
                pool.wait_ge(s_slot2, 1)
                for c in range(C):
                    pool.wait_ge(s_row2[c % RING], 16 * (c // RING + 1))
                    for k in range(TOPK):
                        pool.indirect_dma_start(xs2, bass.IndirectOffsetOnAxis(ap=slot2[:, c, k:k + 1], axis=0),
                                                gbuf[:, c % RING, :], None).then_inc(s_scat2[c], 16)
                zeros_to_xs2(1)
                split_piece(0, 2, SET_E)
                pool.wait_ge(s_down, G_RT)
                for i in range(2):
                    split_piece(1, i, SET_E + 1)
                zeros_to_xs2(2)
                split_piece(1, 2, SET_E + 1)
                zeros_to_xs2(3)

                pool.wait_ge(s_tab2, 1)

                def rest(n, buf, e):
                    pool.wait_ge(s_down, pool.value_load(tab_free[0:1, bass.ds(e, 1)], min_val=G_RT,
                                                         max_val=G_SH2))
                    for i in range(3):
                        split_piece(buf, i, n)
                with pool.Fori(0, (E2 - 2) // 2) as j:
                    rest(SET_E + 2 + 2 * j, 0, 2 * j)
                    rest(SET_E + 3 + 2 * j, 1, 2 * j + 1)
                rest(SET_SH2, 0, E2 - 2)

                for par in range(2):
                    pool.wait_ge(s_yst[par], 16 * stored_before((G_SH2 + (G_SH2 % 2 != par)) // 2, par))
                pool.wait_ge(s_down, G_SH2)
                for c in range(C):
                    if c >= 2:
                        pool.wait_ge(s_cmb, c - 1)
                    for k in range(TOPK):
                        pool.indirect_dma_start(gbuf[:, TOPK * (c % 2) + k, :], None, y2,
                                                bass.IndirectOffsetOnAxis(ap=slot2[:, c, k:k + 1], axis=0)
                                                ).then_inc(s_gy[c % 2], 16)
                    if c == 1:
                        split_piece(1, 0, SET_SH2 + 1)
                        split_piece(1, 1, SET_SH2 + 1)
                    elif c in (3, 5, 7):
                        k = (c - 3) // 2
                        n, (off, _, w), m = SET_SH2 + 1, PIECES[2], CH2[k]
                        cols = slice(off + k * w, off + (k + 1) * w)
                        hi, lo, r = wset[0:m, 1, 0, cols], wset[0:m, 1, 1, cols], raw[0:m, cols]
                        pool.wait_ge(s_raw[2], 32 * (n + 1))
                        pool.tensor_tensor(hi, r, zeros[0:m, 0:1].to_broadcast([m, w]), ALU.add).then_inc(s_pool, 1)
                        pool.wait_ge(s_pool, 3 * n + 3 + k)
                        last = pool.tensor_tensor(lo, r, hi.bitcast(F32), ALU.subtract)
                        if k == 2:
                            last.then_inc(s_split[2], 1)

            @block.scalar
            def _(a):
                def roots(n, tiles):
                    a.wait_ge(s_var, n + 1)
                    a.activation(std[:, 0:tiles], var[:, 0:tiles], ACT.Sqrt).then_inc(s_std, 1)

                def context_hi(n):
                    e, k = n // KD, n % KD
                    a.wait_ge(s_ctp, n + 1)
                    a.activation(ct(e, 0)[:, k, :], ct_banks[n % 4][:], ACT.Copy).then_inc(s_cth, 1)

                for n in range(C // LN):
                    context_hi(n)
                    roots(n, LN)
                    a.wait_ge(s_affine, n + 1)
                    for i in range(LN):
                        a.activation(h_all[:, LN * n + i, :], x_all[:, LN * n + i, :], ACT.Identity,
                                     bias=shift[:, n % 2, i:i + 1], scale=rstd[:, n % 2, i:i + 1]).then_inc(s_h1, 1)

                for n in range(C // LN, E1 * KD):
                    context_hi(n)
                a.wait_ge(s_wrp, 1)
                a.activation(wrT[:, :, 0, :], lg_ps[:, 0:KD * EL].rearrange("p (k e) -> p k e", k=KD),
                             ACT.Copy).then_inc(s_wrhi, 1)

                def load_rows(src, tile, par):
                    a.dma_start(xin[:, par, :].bitcast(F32), src[bass.ds(tile * P, P), :]).then_inc(s_in[par], 16)

                def hi_x(g, par):
                    a.wait_ge(s_xT, g + 1)
                    a.activation(hT[:, par, 0, :], xT_ps[:], ACT.Copy).then_inc(s_hhi, 1)

                def hi_a(g, chunks):
                    a.wait_ge(s_aT, g + 1)
                    if chunks[-1] == P:
                        n = len(chunks) * P
                        a.activation(aT[:, 0, 0:n], aT_ps[:, 0:n], ACT.Copy).then_inc(s_ahi, 1)
                    else:
                        m = chunks[-1]
                        a.activation(aT[:, 0, 0:2 * P], aT_ps[:, 0:2 * P], ACT.Copy)
                        a.activation(aT[0:m, 0, 2 * P:3 * P], aT_ps[0:m, 2 * P:3 * P], ACT.Copy).then_inc(s_ahi, 1)

                def do_silu(g, f):
                    a.wait_ge(s_gate, g + 1)
                    if not (isinstance(g, int) and g == 0):
                        a.wait_ge(s_act, g)
                    a.activation(silu[:, 0:f], g_ps[:, 0:f], ACT.Silu).then_inc(s_silu, 1)

                def y_copy(g, par, before):
                    a.wait_ge(s_down, g + 1)
                    if not (isinstance(before, int) and before == 0):
                        a.wait_ge(s_yst[par], 16 * before)
                    a.activation(ysb[:, par, :], y_ps[:], ACT.Copy).then_inc(s_y, 1)

                def y_store(dst, g, tile, par):
                    a.wait_ge(s_y, g + 1)
                    a.dma_start(dst[bass.ds(tile * P, P), :], ysb[:, par, :]).then_inc(s_yst[par], 16)

                hi_x(0, 0)
                load_rows(xs1, 2, 0)
                do_silu(0, F1)
                hi_x(1, 1)
                load_rows(xs1, 3, 1)

                def layer1(loads, stores):
                    def body(g, half, par):
                        if stores:
                            y_store(y1, g - 2, g - 2, par)
                        hi_a(g - 1, CH1)
                        hi_x(g + 1, 1 - par)
                        if loads:
                            load_rows(xs1, g + 3, 1 - par)
                        do_silu(g, F1)
                        y_copy(g - 1, 1 - par, half - (1 - par))
                    return body
                last = TILES1 - 1
                layer1(True, False)(1, 0, 1)
                layer1(True, True)(2, 1, 0)
                run_steps(a, 3, last - 2, layer1(True, True))
                run_steps(a, last - 2, last, layer1(False, True))
                y_store(y1, last - 2, last - 2, last % 2)
                hi_a(last - 1, CH1)
                do_silu(last, F1)
                hi_a(last, CH1)
                y_copy(last - 1, (last - 1) % 2, (last - 1) // 2)
                y_store(y1, last - 1, last - 1, (last - 1) % 2)
                y_copy(last, last % 2, last // 2)
                y_store(y1, last, last, last % 2)

                first_ln = C // LN
                g = G_SH0
                roots(first_ln, 2)
                hi_x(g, g % 2)
                hi_x(g + 1, 1 - g % 2)
                roots(first_ln + 1, 2)
                do_silu(g, F2)

                def sum_start(c):
                    a.wait_ge(s_down, G_SH0 + c + 1)
                    a.wait_ge(s_h2st[c // 2], 32)
                    a.activation(h_all[:, c, :], y_ps[:], ACT.Copy).then_inc(s_y, 1)

                def load_h2(g, par):
                    load_rows(h2tok, g - G_SH1, par)
                for i in range(1, C + 1):
                    g = G_SH0 + i
                    hi_a(g - 1, CH2)
                    hi_x(g + 1, (g + 1) % 2)
                    if i % 2 == 0 and i <= C - 4:
                        roots(first_ln + i // 2 + 1, 2)
                    if i == C - 3:
                        for j in range(C // 2):
                            a.wait_ge(s_h2st[j], 32)
                    if i >= C - 3:
                        load_h2(g + 3, (g + 3) % 2)
                    do_silu(g, F2)
                    sum_start(i - 1)

                def layer2(first):
                    copies = G_RT <= first - 1 < G_SH2
                    stores = G_RT <= first - 2 < G_SH2
                    row = first + 3
                    src, base = next(((s, b) for s, b, e in (
                        (h2tok, G_SH1, G_RT), (xs2, G_RT, G_SH2), (h2tok, G_SH2, G_SH3),
                        (h2tok, G_SH2, G_SH3), (h2tok, G_SH3, G_END)) if b <= row < e), (None, 0))
                    if row in (G_RT, G_RT + 1):
                        src = None

                    def body(g, half, par):
                        hi_a(g - 1, CH2)
                        if stores:
                            y_store(y2, g - 2, g - 2 - G_RT, par)
                        if first == G_RT - 1:
                            do_silu(g, F2)
                        hi_x(g + 1, 1 - par)
                        if src is not None:
                            load_rows(src, g + 3 - base, 1 - par)
                        if first != G_RT - 1:
                            do_silu(g, F2)
                        if copies:
                            y_copy(g - 1, 1 - par, stored_before(half - (1 - par), 1 - par))
                    return body

                cuts = [G_SH1 + 1, SHARES, G_RT - 3, G_RT - 1, G_RT, G_RT + 1, G_RT + 2,
                        G_RT + ZEROS2[1] - 3, G_RT + ZEROS2[2] - 3, G_SH2 - 3, G_SH2 + 1, G_SH2 + 2,
                        G_SH3 - 3, G_END - 3, G_END - 1]
                assert ZEROS2[0] - 3 == 1
                for first, end in zip(cuts, cuts[1:]):
                    for i in range(1, len(ZEROS2)):
                        if first == G_RT + ZEROS2[i - 1] - 3:
                            a.wait_ge(s_zero2[i], 16 * (ZEROS2[i] - ZEROS2[i - 1]))
                    if first == SHARES:
                        a.wait_ge(s_exin, 1)
                        a.activation(expo[:], expo[:], ACT.Exp).then_inc(s_exp, 1)
                        a.activation(etop[:], etop[:], ACT.Exp).then_inc(s_exp, 1)
                        a.activation(sgate[:], logits[:, :, E2], ACT.Sigmoid).then_inc(s_exp, 1)
                    run_steps(a, first, end, layer2(first))
                g = G_END - 1
                hi_a(g - 1, CH2)
                do_silu(g, F2)
                hi_a(g, CH2)

            @block.tensor
            def _(pe):
                pe.wait_ge(s_const, 10)
                def context(e):
                    pe.wait_ge(s_ctx[e], 16)
                    for k in range(KD):
                        n = e * KD + k
                        if n >= 4:
                            pe.wait_ge(s_ctl, n - 3)
                        for f in range(KD):
                            last = pe.transpose(ct_banks[n % 4][:, f * P:(f + 1) * P],
                                                raw_ctx(e)[:, f, k * P:(k + 1) * P], ident[:])
                        last.then_inc(s_ctp, 1)

                def ranks(width, s_mask, s_cum):
                    pe.wait_ge(s_mask, 1)
                    pe.matmul(cum_ps[:, 0:width], tri[:], maskb[:, 0:width], start=True, stop=True)
                    pe.matmul(tot_ps[:, 0:width], ones[:], maskb[:, 0:width], start=True,
                              stop=True).then_inc(s_cum, 1)
                ranks(C * E1, s_mask1, s_cum1)
                for e in range(E1):
                    context(e)

                def warm_up(n, moving):
                    for i in range(n):
                        pe.matmul(tot_ps[:], ident_r[:], moving, start=True, stop=True)

                pe.wait_ge(s_wr, 32)
                for k in range(KD):
                    last = pe.transpose(lg_ps[:, k * EL:(k + 1) * EL], wr_rows[:, k * P:(k + 1) * P],
                                        ident[0:EL, 0:EL])
                last.then_inc(s_wrp, 1)

                def x_transposes(g, half, par, skipped=0):
                    pe.wait_ge(s_in[par], 16 * (half + 1 - skipped))
                    if not (isinstance(g, int) and g == 0):
                        pe.wait_ge(s_hT, g)
                    for k in range(KD):
                        last = pe.transpose(xT_ps[:, k * P:(k + 1) * P].bitcast(F32R), xin[:, par, k * P:(k + 1) * P],
                                            ident_r[:])
                    last.then_inc(s_xT, 1)

                def a_transposes(g, chunks):
                    pe.wait_ge(s_act, g + 1)
                    for k, m in enumerate(chunks):
                        last = pe.transpose(aT_ps[0:m, k * P:(k + 1) * P], act[:, k * P:k * P + m], ident[:])
                    last.then_inc(s_aT, 1)

                def product(ps, left, right, chunks, done):
                    n = 3 * len(chunks)
                    i = 0
                    for k, m in enumerate(chunks):
                        for l, r in ((0, 0), (0, 1), (1, 0)):
                            mm = pe.matmul(ps, left(l, k, m), right(r, k, m), start=(i == 0), stop=(i == n - 1))
                            i += 1
                    mm.then_inc(done, 1)

                def h_left(par):
                    return lambda l, k, m: hT[0:m, par, l, k * P:(k + 1) * P]

                def a_left(l, k, m):
                    return aT[0:m, l, k * P:(k + 1) * P]

                def context_of(g):
                    at = pe.value_load(tab1[0:1, bass.ds(g, 1)], min_val=0, max_val=2 * WSET + KD * F1)
                    return lambda r, k, m: wflat[:, bass.ds(at + (r * WSET + k * F1), F1)]

                def down1(g, right):
                    pe.wait_ge(s_aTs, g + 1)
                    if not (isinstance(g, int) and g == 0):
                        pe.wait_ge(s_y, g)
                    product(y_ps[:], a_left, right, CH1, s_down)

                def gate1(g, par, right):
                    pe.wait_ge(s_hT, g + 1)
                    product(g_ps[:], h_left(par), right, CH1, s_gate)

                pe.wait_ge(s_slot1, 1)
                warm_up(5, ct(0, 0)[:, 0, :])
                pe.wait_ge(s_ctl, E1 * KD)
                first = context_of(0)
                x_transposes(0, 0, 0)
                warm_up(3, ct(0, 0)[:, 0, :])
                gate1(0, 0, first)
                x_transposes(1, 0, 1)

                def layer1(g, half, par):
                    own, before = context_of(g), context_of(g - 1)
                    a_transposes(g - 1, CH1)
                    x_transposes(g + 1, half + (1 if par else 0), 1 - par)
                    gate1(g, par, own)
                    down1(g - 1, before)
                layer1(1, 0, 1)
                run_steps(pe, 2, TILES1 - 1, layer1)
                g = TILES1 - 1
                own, before = context_of(g), context_of(g - 1)
                a_transposes(g - 1, CH1)
                gate1(g, g % 2, own)
                down1(g - 1, before)
                a_transposes(g, CH1)
                warm_up(5, ct(E1 - 1, 0)[:, 0, :])
                down1(g, own)

                def set_right(at, part):
                    off, _, w = PIECES[part]
                    return lambda r, k, m: wflat[0:m, bass.ds(at + (r * WSET + off + k * w), w)]

                def gate_up(g, par, at, number):
                    pe.wait_ge(s_hT, g + 1)
                    pe.wait_ge(s_split[0], number)
                    product(g_ps[:, 0:F2], h_left(par), set_right(at, 0), [P] * KD, s_gate)
                    pe.wait_ge(s_split[1], number)
                    pe.wait_ge(s_split[2], number)
                    product(u_ps[:, 0:F2], h_left(par), set_right(at, 1), [P] * KD, s_up)

                def down2(g, at):
                    pe.wait_ge(s_aTs, g + 1)
                    pe.wait_ge(s_y, g)
                    product(y_ps[:], a_left, set_right(at, 2), CH2, s_down)

                def h_transposes(c):
                    pe.wait_ge(s_h2, c + 1)
                    pe.wait_ge(s_hT, G_SH0 + c)
                    for k in range(KD):
                        last = pe.transpose(xT_ps[:, k * P:(k + 1) * P], h_all[:, c, k * P:(k + 1) * P], ident[:])
                    last.then_inc(s_xT, 1)

                def router_product(c, par):
                    if c >= 2:
                        pe.wait_ge(s_lgs, c - 1)
                    bank = lg_banks[c % 2]
                    for k in range(KD):
                        pe.matmul(bank[:, 0:2 * EL], h_left(par)(0, k, P), wrT[:, k, :, :], start=(k == 0), stop=False)
                        last = pe.matmul(bank[:, 0:EL], h_left(par)(1, k, P), wrT[:, k, 0, :], start=False,
                                         stop=(k == KD - 1))
                    last.then_inc(s_lg, 1)

                skipped = C // 2
                g = G_SH0
                pe.wait_ge(s_wrT, 1)
                pe.wait_ge(s_g1[0], 16)
                pe.wait_ge(s_split[0], 1)
                gate_row = wset[:, 0, 0, 0:512]
                warm_up(8, gate_row)
                h_transposes(0)
                warm_up(5, gate_row)
                h_transposes(1)
                gate_up(g, g % 2, 0, 1)
                router_product(0, g % 2)
                for c in range(1, C):
                    g = G_SH0 + c
                    a_transposes(g - 1, CH2)
                    if c < C - 1:
                        h_transposes(c + 1)
                    else:
                        x_transposes(g + 1, (g + 1) // 2, (g + 1) % 2, skipped)
                    gate_up(g, g % 2, 0, 1)
                    router_product(c, g % 2)
                    down2(g - 1, 0)

                def in_set(at, number, before):
                    def body(g, half, par):
                        a_transposes(g - 1, CH2)
                        x_transposes(g + 1, half + (1 if par else 0), 1 - par, skipped)
                        gate_up(g, par, at, number)
                        down2(g - 1, before)
                    return body
                odd, even = 2 * WSET, 0
                g = G_SH1
                in_set(odd, 2, even)(g, g // 2, g % 2)
                g = G_SH1 + 1
                a_transposes(g - 1, CH2)
                x_transposes(g + 1, (g + 1) // 2, (g + 1) % 2, skipped)
                gate_up(g, g % 2, odd, 2)
                ranks(C * E2, s_mask2, s_cum2)
                down2(g - 1, odd)
                run_steps(pe, G_SH1 + 2, G_RT - 1, in_set(odd, 2, odd))
                def set_of(row):
                    return (pe.value_load(tab_buf[0:1, bass.ds(row + 1, 1)], min_val=0, max_val=2 * WSET),
                            pe.value_load(tab_cnt[0:1, bass.ds(row, 1)], min_val=1, max_val=SET_SH2),
                            pe.value_load(tab_buf[0:1, bass.ds(row, 1)], min_val=0, max_val=2 * WSET))

                g = G_RT - 1
                a_transposes(g - 1, CH2)
                gate_up(g, g % 2, odd, 2)
                x_transposes(g + 1, (g + 1) // 2, (g + 1) % 2, skipped)
                down2(g - 1, odd)

                def by_table(g, half, par):
                    in_set(*set_of(g - G_RT))(g, half, par)
                pe.wait_ge(s_tab2, 1)
                run_steps(pe, G_RT, G_SH2, by_table)
                g = G_SH2
                before = pe.value_load(tab_buf[0:1, TILES2:TILES2 + 1], min_val=0, max_val=2 * WSET)
                in_set(even, SET_SH2 + 1, before)(g, g // 2, g % 2)
                run_steps(pe, G_SH2 + 1, G_SH3, in_set(even, SET_SH2 + 1, even))
                g = G_SH3
                in_set(odd, SET_SH2 + 2, even)(g, g // 2, g % 2)
                run_steps(pe, G_SH3 + 1, G_END - 1, in_set(odd, SET_SH2 + 2, odd))
                g = G_END - 1
                a_transposes(g - 1, CH2)
                gate_up(g, g % 2, odd, SET_SH2 + 2)
                down2(g - 1, odd)
                a_transposes(g, CH2)
                down2(g, odd)

            @block.vector
            def _(v):
                chained = [0]

                def step(ins):
                    chained[0] += 1
                    ins.then_inc(s_dve, 1)
                    v.wait_ge(s_dve, chained[0])

                def link(ins, k):
                    ins.then_inc(s_ln, 1)
                    v.wait_ge(s_ln, k)

                def variances(n, tiles):
                    for i in range(tiles):
                        last = v.bn_aggr(mv[:, i, :], stats[:, i, :])
                    link(last, 7 * n + 2)
                    v.tensor_scalar(var[:, 0:tiles], mv[:, 0:tiles, 1], EPS, None, ALU.add).then_inc(s_var, 1)

                def deviations(n, tiles):
                    r, t, w = rstd[:, n % 2, 0:tiles], newton[:, 0:tiles], var[:, 0:tiles]
                    v.wait_ge(s_std, n + 1)
                    link(v.reciprocal(r, std[:, 0:tiles]), 7 * n + 3)
                    link(v.tensor_tensor(t, r, r, ALU.mult), 7 * n + 4)
                    link(v.tensor_tensor(t, t, w, ALU.mult), 7 * n + 5)
                    link(v.tensor_scalar(t, t, -0.5, 1.5, ALU.mult, ALU.add), 7 * n + 6)
                    link(v.tensor_tensor(r, r, t, ALU.mult), 7 * n + 7)

                def slots(E, s_cum):
                    W = C * E
                    v.wait_ge(s_cum, 1)
                    tot_e = tot[:, 0:W].rearrange("p (e c) -> p e c", e=E)
                    step(v.tensor_copy(tot_e, tot_ps[:, 0:W].rearrange("p (c e) -> p e c", e=E)))
                    step(v.tensor_reduce(cnt[:, 0:E], tot_e, AX.X, ALU.add))
                    step(v.tensor_scalar(padi[:, 0:E], cnt[:, 0:E], 1.0, float(P - 1), ALU.max, ALU.add))
                    step(v.tensor_scalar(padi[:, 0:E], padi[:, 0:E], 7, 7, ALU.arith_shift_right,
                                         ALU.arith_shift_left))
                    step(v.tensor_copy(padf[:, 0:E], padi[:, 0:E]))
                    step(v.tensor_tensor_scan(bend[:, 0:E], one_row[:, 0:E], padf[:, 0:E], 0.0, ALU.mult, ALU.add))
                    step(v.tensor_tensor_scan(cexc[:, 0:E], one_row[:, 0:E], cnt[:, 0:E], 0.0, ALU.mult, ALU.add))
                    step(v.tensor_tensor(cexc[:, 0:E], bend[:, 0:E], cexc[:, 0:E], ALU.subtract))
                    step(v.tensor_tensor(cexc[:, 0:E], cexc[:, 0:E], padf[:, 0:E], ALU.subtract))
                    step(v.tensor_tensor(cexc[:, 0:E], cexc[:, 0:E], cnt[:, 0:E], ALU.add))

                def slots_end(E):
                    W = C * E
                    run_e = run[:, 0:W].rearrange("p (e c) -> p e c", e=E)
                    step(v.tensor_tensor_scan(run[:, 0:W], one_row[:, 0:W], tot[:, 0:W], 0.0, ALU.mult, ALU.add))
                    step(v.tensor_tensor(run[:, 0:W], run[:, 0:W], tot[:, 0:W], ALU.subtract))
                    step(v.tensor_tensor(run_e, run_e, cexc[:, 0:E].unsqueeze(2).to_broadcast([P, E, C]), ALU.add))
                    step(v.tensor_tensor(vslot[:, :, 0:E], cum_ps[:, 0:W].rearrange("p (c e) -> p c e", e=E),
                                         run[:, 0:W].rearrange("p (e c) -> p c e", e=E), ALU.add))

                def free_slots(E, tiles, to, done):
                    shape = [P, tiles, E]
                    cmp, count = cmp_t[:, 0:tiles, 0:E], freef[:, 0:tiles]
                    step(v.tensor_tensor(cmp, cexc[:, 0:E].unsqueeze(1).to_broadcast(shape),
                                         iota_free[:, 0:tiles].unsqueeze(2).to_broadcast(shape), ALU.is_le))
                    step(v.tensor_tensor(cmp, cmp, cnt[:, 0:E].unsqueeze(1).to_broadcast(shape), ALU.mult))
                    step(v.tensor_reduce(count, cmp, AX.X, ALU.add))
                    step(v.tensor_tensor(count, count, iota_free[:, 0:tiles], ALU.add))
                    v.tensor_copy(to[:], count).then_inc(done, 1)

                def tile_ends(E):
                    step(v.tensor_scalar(bend[:, 0:E], bend[:, 0:E], 1.0 / P, None, ALU.mult))

                def experts_of_tiles(E, t0, t1):
                    cmp = cmp_t[:, 0:t1 - t0, 0:E]
                    step(v.tensor_tensor(cmp, bend[:, 0:E].unsqueeze(1).to_broadcast([P, t1 - t0, E]),
                                         iota_t[:, t0:t1].unsqueeze(2).to_broadcast([P, t1 - t0, E]), ALU.is_le))
                    step(v.tensor_reduce(texp[:, t0:t1], cmp, AX.X, ALU.add))
                    step(v.tensor_scalar(texp[:, t0:t1], texp[:, t0:t1], float(E - 1), None, ALU.min))

                one_row = expo[:].rearrange("p c e -> p (c e)")
                step(v.memset(one_row, 1.0))

                v.wait_ge(s_tok, 16)
                hot1 = hot[:, 0, :, 0:E1]
                ge = hot[:, 1, :, 0:E1 + 1]
                step(v.memset(ge[:, :, 0], 1.0))
                step(v.memset(ge[:, :, E1], 0.0))
                for e in range(1, E1):
                    step(v.tensor_scalar(ge[:, :, e], tokid[:], float(BOUND1 * e), None, ALU.is_ge))
                step(v.tensor_tensor(hot1, ge[:, :, 0:E1], ge[:, :, 1:E1 + 1], ALU.subtract))
                v.tensor_copy(maskb[:, 0:C * E1].rearrange("p (c e) -> p c e", e=E1), hot1).then_inc(s_mask1, 1)
                v.wait_ge(s_const, 10)
                slots(E1, s_cum1)
                slots_end(E1)
                free_slots(E1, FREE1, free1, s_free1)
                tile_ends(E1)
                experts_of_tiles(E1, 0, TILES1)
                step(v.tensor_scalar(late[:], texp[0:1, 0:TILES1], 2.0, float(2 * WSET - 2 * KD * F1), ALU.is_ge,
                                     ALU.mult))
                step(v.scalar_tensor_tensor(out=tab1[:], in0=texp[0:1, 0:TILES1], scalar=float(KD * F1), in1=late[:],
                                            op0=ALU.mult, op1=ALU.add))
                step(v.tensor_copy(tab_ct[:], bend[0:1, 1:2]))
                step(v.tensor_tensor(vslot[:, :, 0:E1], vslot[:, :, 0:E1], hot1, ALU.mult))
                step(v.tensor_reduce(slotf[:, :, 0], vslot[:, :, 0:E1], AX.X, ALU.add))
                v.tensor_copy(slot1[:], slotf[:, :, 0]).then_inc(s_slot1, 1)

                def context_lo(n):
                    e, k = n // KD, n % KD
                    v.wait_ge(s_cth, n + 1)
                    v.tensor_tensor(ct(e, 1)[:, k, :], ct_banks[n % 4][:], ct(e, 0)[:, k, :].bitcast(F32),
                                    ALU.subtract).then_inc(s_ctl, 1)

                for n in range(C // LN):
                    v.wait_ge(s_x[n], 16)
                    for i in range(LN):
                        last = v.bn_stats(stats[:, i, :], x_all[:, LN * n + i, :])
                    link(last, 7 * n + 1)
                    variances(n, LN)
                    context_lo(n)
                    if n >= 2:
                        v.wait_ge(s_h1, LN * (n - 1))
                    deviations(n, LN)
                    v.scalar_tensor_tensor(out=shift[:, n % 2], in0=mv[:, :, 0], scalar=-1.0, in1=rstd[:, n % 2],
                                           op0=ALU.mult, op1=ALU.mult).then_inc(s_affine, 1)
                for n in range(C // LN, E1 * KD):
                    context_lo(n)
                v.wait_ge(s_wrhi, 1)
                v.tensor_tensor(wrT[:, :, 1, :], lg_ps[:, 0:KD * EL].rearrange("p (k e) -> p k e", k=KD),
                                wrT[:, :, 0, :].bitcast(F32), ALU.subtract).then_inc(s_wrT, 1)

                def lo_x(g, par):
                    v.wait_ge(s_hhi, g + 1)
                    v.tensor_tensor(hT[:, par, 1, :], xT_ps[:], hT[:, par, 0, :].bitcast(F32),
                                    ALU.subtract).then_inc(s_hT, 1)

                def lo_a(g, chunks):
                    v.wait_ge(s_ahi, g + 1)
                    if chunks[-1] == P:
                        n = len(chunks) * P
                        v.tensor_tensor(aT[:, 1, 0:n], aT_ps[:, 0:n], aT[:, 0, 0:n].bitcast(F32),
                                        ALU.subtract).then_inc(s_aTs, 1)
                    else:
                        m = chunks[-1]
                        v.tensor_tensor(aT[:, 1, 0:2 * P], aT_ps[:, 0:2 * P], aT[:, 0, 0:2 * P].bitcast(F32),
                                        ALU.subtract)
                        v.tensor_tensor(aT[0:m, 1, 2 * P:3 * P], aT_ps[0:m, 2 * P:3 * P],
                                        aT[0:m, 0, 2 * P:3 * P].bitcast(F32), ALU.subtract).then_inc(s_aTs, 1)

                def act1(g):
                    v.wait_ge(s_silu, g + 1)
                    v.tensor_tensor(act[:], g_ps[:], silu[:], ALU.mult).then_inc(s_act, 1)

                def act2(g):
                    v.wait_ge(s_silu, g + 1)
                    v.wait_ge(s_up, g + 1 - TILES1)
                    v.tensor_tensor(act[:, 0:F2], u_ps[:, 0:F2], silu[:, 0:F2], ALU.mult).then_inc(s_act, 1)

                lo_x(0, 0)
                act1(0)
                lo_x(1, 1)

                def layer1(g, half, par):
                    lo_a(g - 1, CH1)
                    lo_x(g + 1, 1 - par)
                    act1(g)
                run_steps(v, 1, TILES1 - 1, layer1)
                g = TILES1 - 1
                lo_a(g - 1, CH1)
                act1(g)
                lo_a(g, CH1)

                first_ln = C // LN
                def residual(c):
                    v.wait_ge(s_g1[c % RING], 16 * (c // RING + 1))
                    v.tensor_tensor(x_all[:, c, :], x_all[:, c, :], gbuf[:, c % RING, :], ALU.add).then_inc(s_x1, 1)
                    v.wait_ge(s_x1, c + 1)
                    last = v.bn_stats(stats[:, c % 2, :], x_all[:, c, :])
                    if c % 2:
                        link(last, 7 * (first_ln + c // 2) + 1)

                def rows(j):
                    deviations(first_ln + j, 2)
                    for i in range(2):
                        v.tensor_scalar(h_all[:, 2 * j + i, :], x_all[:, 2 * j + i, :], mv[:, i, 0:1],
                                        rstd[:, (first_ln + j) % 2, i:i + 1], ALU.subtract,
                                        ALU.mult).then_inc(s_h2, 1)

                def top(c):
                    v.wait_ge(s_lg, c + 1)
                    bank = lg_banks[c % 2]
                    step(v.tensor_copy(logits[:, c, :], bank[:, 0:EL]))
                    v.tensor_tensor(logits[:, c, :], logits[:, c, :], bank[:, EL:2 * EL], ALU.add).then_inc(s_lgs, 1)
                    v.wait_ge(s_lgs, c + 1)
                    step(v.max(top8[:, c, :], logits[:, c, 0:E2]))
                    v.max_index(idx8[:, c, :], top8[:, c, :], logits[:, c, 0:E2]).then_inc(s_top, 1)

                g = G_SH0
                residual(0)
                residual(1)
                variances(first_ln, 2)
                rows(0)
                residual(2)
                lo_x(g, g % 2)
                residual(3)
                variances(first_ln + 1, 2)
                lo_x(g + 1, 1 - g % 2)
                rows(1)
                act2(g)
                for i in range(1, C):
                    g = G_SH0 + i
                    lo_a(g - 1, CH2)
                    lo_x(g + 1, 1 - g % 2)
                    if i % 2 == 0 and i <= C - 4:
                        rows(i // 2 + 1)
                    act2(g)
                    if i % 2 and i <= C - 5:
                        j = (i + 3) // 2
                        residual(2 * j)
                        residual(2 * j + 1)
                        variances(first_ln + j, 2)
                    top(i - 1)

                def add_y(g, c):
                    v.wait_ge(s_down, g + 1)
                    v.tensor_tensor(tile_of(h_all, c), y_ps[:], tile_of(h_all, c), ALU.add).then_inc(s_y, 1)

                def masks():
                    v.wait_ge(s_top, C)
                    step(v.tensor_copy(idxf[:], idx8[:, :, 0:TOPK]))
                    for k in range(TOPK):
                        last = v.tensor_tensor(hot[:, k], iota_e[:].unsqueeze(1).to_broadcast([P, C, E2]),
                                               idxf[:, :, k:k + 1].to_broadcast([P, C, E2]), ALU.is_equal)
                    step(last)
                    step(v.tensor_tensor(vslot[:], hot[:, 0], hot[:, 1], ALU.add))
                    step(v.tensor_tensor(vslot[:], vslot[:], hot[:, 2], ALU.add))
                    v.tensor_tensor(maskb[:].rearrange("p (c e) -> p c e", e=E2), vslot[:], hot[:, 3],
                                    ALU.add).then_inc(s_mask2, 1)

                def slots_of_choices():
                    step(v.tensor_tensor(hot, hot, vslot[:].unsqueeze(1).to_broadcast([P, TOPK, C, E2]), ALU.mult))
                    step(v.tensor_reduce(slotf[:].rearrange("p c k -> p k c"), hot, AX.X, ALU.add))
                    v.tensor_copy(slot2[:], slotf[:]).then_inc(s_slot2, 1)

                def tables():
                    sets = slice(1, 1 + TILES2)
                    step(v.memset(tab_buf[:, 0:1], 2 * WSET))
                    step(v.tensor_scalar(tab_cnt[:, 0:TILES2], texp[0:1, :], float(SET_E + 1), None, ALU.add))
                    step(v.tensor_copy(texi[0:1, :], texp[0:1, :]))
                    step(v.tensor_scalar(texi[0:1, :], texi[0:1, :], 1, None, ALU.bitwise_and))
                    step(v.tensor_scalar(tab_buf[:, sets], texi[0:1, :], float(2 * WSET), None, ALU.mult))
                    v.tensor_scalar(tab_free[:], bend[0:1, :], float(G_RT), None, ALU.add).then_inc(s_tab2, 1)

                def exponents():
                    step(v.tensor_tensor(etop[:], top8[:, :, 0:TOPK], top8[:, :, 0:1].to_broadcast([P, C, TOPK]),
                                         ALU.subtract))
                    v.tensor_tensor(expo[:], logits[:, :, 0:E2], top8[:, :, 0:1].to_broadcast([P, C, E2]),
                                    ALU.subtract).then_inc(s_exin, 1)

                def shares():
                    v.wait_ge(s_exp, 3)
                    step(v.tensor_reduce(zsum[:], expo[:], AX.X, ALU.add))
                    step(v.reciprocal(zsum[:], zsum[:]))
                    step(v.tensor_tensor(etop[:], etop[:], zsum[:].unsqueeze(2).to_broadcast([P, C, TOPK]), ALU.mult))
                    step(v.tensor_reduce(zsum[:], etop[:], AX.X, ALU.add))
                    step(v.tensor_scalar(zsum[:], zsum[:], 1e-9, None, ALU.max))
                    step(v.reciprocal(zsum[:], zsum[:]))
                    step(v.tensor_tensor(combw[:], etop[:], zsum[:].unsqueeze(2).to_broadcast([P, C, TOPK]), ALU.mult))

                def halves(g, par):
                    lo_a(g - 1, CH2)
                    lo_x(g + 1, 1 - par)
                    act2(g)

                g = G_SH1
                halves(g, g % 2)
                top(C - 1)
                masks()
                for i in range(1, SHARES - G_SH1 + 1):
                    g = G_SH1 + i
                    halves(g, g % 2)
                    if i == 1:
                        slots(E2, s_cum2)
                    elif i == 2:
                        free_slots(E2, FREE2, free2, s_free2)
                    add_y(g - 1, i - 1)
                    if i == 1:
                        slots_end(E2)
                    elif i == 2:
                        slots_of_choices()
                    elif i == 3:
                        tile_ends(E2)
                        experts_of_tiles(E2, 0, TILES2 // 2)
                    elif i == 4:
                        experts_of_tiles(E2, TILES2 // 2, TILES2)
                    elif i == 5:
                        tables()
                    elif i == 6:
                        exponents()
                    elif g == SHARES:
                        shares()

                def with_sum(c0):
                    def body(g, half, par):
                        halves(g, par)
                        add_y(g - 1, g - c0)
                    return body
                run_steps(v, SHARES + 1, G_RT - 1, with_sum(G_SH1 + 1))
                g = G_RT - 1
                lo_a(g - 1, CH2)
                act2(g)
                lo_x(g + 1, (g + 1) % 2)
                add_y(g - 1, C - 2)
                halves(G_RT, G_RT % 2)
                add_y(G_RT - 1, C - 1)

                run_steps(v, G_RT + 1, G_SH2 + 1, lambda g, half, par: halves(g, par))

                def combine(c, par, turn, ks):
                    if ks[0] == 0:
                        v.wait_ge(s_gy[par], 16 * TOPK * (turn + 1))
                    row = tile_of(x_all, c)
                    for k in ks:
                        if k:
                            v.wait_ge(s_cstep, 3 * c + k)
                        ins = v.scalar_tensor_tensor(
                            out=row, in0=gbuf[:, TOPK * par + k, :],
                            scalar=combw[:, bass.ds(c, 1), k:k + 1].rearrange("p a k -> p (a k)"),
                            in1=row, op0=ALU.mult, op1=ALU.add)
                        ins.then_inc(s_cmb if k == TOPK - 1 else s_cstep, 1)

                run_steps(v, G_SH2 + 1, COMBINE, with_sum(G_SH2 + 1))
                ahead = COMBINE - G_SH2 - 1

                def combining(c, par, turn, result):
                    g, gpar = COMBINE + c, (COMBINE + par) % 2
                    lo_a(g - 1, CH2)
                    lo_x(g + 1, 1 - gpar)
                    if not (isinstance(c, int) and c == 0):
                        combine(c - 1, 1 - par, None, (3,))
                    act2(g)
                    combine(c, par, turn, (0,))
                    result()
                    combine(c, par, turn, (1, 2))

                def summing(c, par, turn):
                    combining(c, par, turn, lambda: add_y(COMBINE - 1 + c, ahead + c))
                n = (C - ahead - 1) // 2
                summing(0, 0, 0)
                with v.Fori(0, n) as j:
                    for u in range(2):
                        summing(1 + u + 2 * j, (1 + u) % 2, j + (1 + u) // 2)
                for c in range(1 + 2 * n, C - ahead):
                    summing(c, c % 2, c // 2)

                def last_out(g, c):
                    v.wait_ge(s_y, g + 1)
                    gate = sgate[:, c:c + 1] if isinstance(c, int) else sgate[:, bass.ds(c, 1)]
                    row = tile_of(x_all, c)
                    v.scalar_tensor_tensor(out=row, in0=tile_of(h_all, c), scalar=gate, in1=row, op0=ALU.mult,
                                           op1=ALU.add).then_inc(s_fin, 1)

                def last_sum(g, c):
                    add_y(g, c)
                    last_out(g, c)

                for c in range(C - ahead, C):
                    combining(c, c % 2, c // 2, lambda: last_sum(COMBINE - 1 + c, c - C + ahead))
                def final(g, half, par):
                    halves(g, par)
                    last_sum(g - 1, g - 1 - G_SH3)
                final(G_SH3 + 1 + ahead, None, (G_SH3 + 1 + ahead) % 2)
                combine(C - 1, (C - 1) % 2, None, (3,))
                run_steps(v, G_SH3 + 2 + ahead, G_END - 1, final)
                g = G_END - 1
                lo_a(g - 1, CH2)
                act2(g)
                add_y(g - 1, C - 2)
                lo_a(g, CH2)
                last_out(g - 1, C - 2)
                last_sum(g, C - 1)


_INS = ["x", "itok_BxS_13_99985", "ctx_2048", "L0_ffn_router_w", "L0_ffn_w_gate", "L0_ffn_w_up", "L0_ffn_w_down",
        "L0_ffn_sh_gate", "L0_ffn_sh_up", "L0_ffn_sh_down", "L0_ffn_sh_gate_w"]

_OUTS = [((4, 512, 512), "float32")]


def kernel(**inputs):
    import numpy as _np
    import concourse.bacc as _bacc
    from concourse import mybir as _mybir
    from concourse.bass_utils import run_bass_kernel_spmd as _run

    nc = _bacc.Bacc("TRN2", target_bir_lowering=False, num_devices=1)
    arrays, args = {}, []
    for name in _INS:
        a = _np.ascontiguousarray(inputs[name])
        arrays[f"in_{name}_dram"] = a
        args.append(nc.dram_tensor(f"in_{name}_dram", a.shape, _mybir.dt.from_np(a.dtype), kind="ExternalInput").ap())
    for i, (shape, dtype) in enumerate(_OUTS):
        dt = _mybir.dt.from_np(_np.dtype(dtype))
        args.append(nc.dram_tensor(f"out_{i}_dram", shape, dt, kind="ExternalOutput").ap())
    build(nc, *args)
    r = _run(nc, [arrays], core_ids=[0])
    return r.results[0]["out_0_dram"]
```
